# Optimizing a Trainium2 kernel written in Bass

```python
import numpy as np
import jax
import jax.numpy as jnp

def _softmax(x, axis=-1):
    return jax.nn.softmax(x, axis=axis)

def _gelu(x):
    return jax.nn.gelu(x, approximate=True)

def _silu(x):
    return jax.nn.silu(x)

def _sigmoid(x):
    return jax.nn.sigmoid(x)

def _layernorm(x, axis=-1, eps=1e-05):
    m = jnp.mean(x, axis=axis, keepdims=True)
    v = jnp.var(x, axis=axis, keepdims=True)
    return (x - m) / jnp.sqrt(v + eps)

def _scatter_add(tgt, idx, src, axis=0):
    return tgt.at[idx].add(src)

def _segment_sum(src, seg, n):
    return jax.ops.segment_sum(src, seg, n)
kernel_name = 'mk_audio_tower_d1_tok_audfeat256_r4_2fc61b'

def setup_inputs(seed: int=0):
    np.random.seed(seed)
    _w = jnp.asarray

    def _rec_inputs():
        import jax
        import jax.numpy as jnp
        _rk = jax.random.key(seed)
        x = -0.000520686 + 1.00062 * jax.random.normal(jax.random.fold_in(_rk, 1), (64, 125, 64), jnp.float32)
        return x
    x = _rec_inputs()

    def _L0_tok_setup():
        import jax, jax.numpy as jnp
        import numpy as np
        BATCH = 2
        SEQ = 1024
        D_MODEL = 64
        N_STATE = 64
        DT_RANK = 1
        NUM_LAYERS = 3

        def _ssm_layer(x, A_log, Dp, W_dbc, W_dt, b_dt):
            A = -jnp.exp(A_log)
            dbc = jnp.einsum('ble,ce->blc', x, W_dbc)
            delta, Bm, Cm = jnp.split(dbc, [DT_RANK, DT_RANK + N_STATE], axis=-1)
            delta = jax.nn.softplus(jnp.einsum('blr,er->ble', delta, W_dt) + b_dt)
            dA = jnp.exp(delta[..., None] * A)
            dBx = (delta * x)[..., None] * Bm[:, :, None, :]

            def combine(c1, c2):
                a1, h1 = c1
                a2, h2 = c2
                return (a1 * a2, h1 * a2 + h2)
            _, hs = jax.lax.associative_scan(combine, (dA, dBx), axis=1)
            y = jnp.einsum('blen,bln->ble', hs, Cm)
            return y + Dp * x
        key = jax.random.key(seed)
        kx, kw1, kw2 = jax.random.split(key, 3)
        x = jax.random.normal(kx, (BATCH, SEQ, D_MODEL), dtype=jnp.float32)
        A_log = jnp.broadcast_to(jnp.log(jnp.arange(1, N_STATE + 1, dtype=jnp.float32)), (NUM_LAYERS, D_MODEL, N_STATE)).copy()
        D = jnp.ones((NUM_LAYERS, D_MODEL), dtype=jnp.float32)
        W_dbc = 0.02 * jax.random.normal(kw1, (NUM_LAYERS, DT_RANK + 2 * N_STATE, D_MODEL), dtype=jnp.float32)
        W_dt = 0.02 * jax.random.normal(kw2, (NUM_LAYERS, D_MODEL, DT_RANK), dtype=jnp.float32)
        b_dt = jnp.zeros((NUM_LAYERS, D_MODEL), dtype=jnp.float32)
        return {'x': x, 'A_log': A_log, 'D': D, 'W_dbc': W_dbc, 'W_dt': W_dt, 'b_dt': b_dt}
    _L0_tok_all = _L0_tok_setup()
    _L0_tok_in = {k: v for k, v in _L0_tok_all.items() if k in ('A_log', 'D', 'W_dbc', 'W_dt', 'b_dt')}
    del _L0_tok_all

    def _L0_attn_setup():
        import jax, jax.numpy as jnp
        import numpy as np
        D_MODEL = 64
        N_HEAD = 8

        def _l1_scores(q, k):
            scale = 1.0 / np.sqrt(q.shape[-1]).astype(np.float32)
            q_sbhw = q.transpose(1, 0, 2, 3)

            def one_query(qs):
                return -jnp.sum(jnp.abs(qs[:, None, :, :] - k), axis=-1) * scale
            s = jax.lax.map(one_query, q_sbhw)
            return s.transpose(1, 0, 2, 3)
        key = jax.random.key(seed)
        ks = jax.random.split(key, 3)
        b, t = (4, 250)
        x = jax.random.normal(ks[0], (b, t, D_MODEL), jnp.float32)
        wqv_w = 0.005 * jax.random.normal(ks[1], (3 * N_HEAD * D_MODEL, D_MODEL), jnp.float32)
        wqv_b = jnp.zeros((3 * N_HEAD * D_MODEL,), jnp.float32)
        wk = 0.005 * jnp.ones((N_HEAD, D_MODEL), jnp.float32)
        fanin_w = 0.005 * jax.random.normal(ks[2], (D_MODEL, D_MODEL), jnp.float32)
        fanin_b = jnp.zeros((D_MODEL,), jnp.float32)
        return dict(x=x, wqv_w=wqv_w, wqv_b=wqv_b, wk=wk, fanin_w=fanin_w, fanin_b=fanin_b)
    _L0_attn_all = _L0_attn_setup()
    _L0_attn_in = {k: v for k, v in _L0_attn_all.items() if k in ('wqv_w', 'wqv_b', 'wk', 'fanin_w', 'fanin_b')}
    del _L0_attn_all

    def _L0_ffn_setup():
        import jax, jax.numpy as jnp
        import numpy as np
        E, D, H, TOP_K = (6, 64, 64, 2)
        ROUTER_H = D // 2
        key = jax.random.key(seed)
        ks = jax.random.split(key, 12)
        s = 1.0 / np.sqrt(D)
        sh = 1.0 / np.sqrt(H)
        sr = 1.0 / np.sqrt(ROUTER_H)
        return {'features': jax.random.normal(ks[0], (8, 1024, D), dtype=jnp.float32), 'router_w1': jax.random.uniform(ks[1], (D, ROUTER_H), jnp.float32, -s, s), 'router_b1': jnp.zeros((ROUTER_H,), jnp.float32), 'router_w2': jax.random.uniform(ks[2], (ROUTER_H, E), jnp.float32, -sr, sr), 'router_b2': jnp.zeros((E,), jnp.float32), 'expert_w1': jax.random.uniform(ks[3], (E, D, H), jnp.float32, -s, s), 'expert_b1': jnp.zeros((E, H), jnp.float32), 'expert_w2': jax.random.uniform(ks[4], (E, H, H), jnp.float32, -sh, sh), 'expert_b2': jnp.zeros((E, H), jnp.float32), 'expert_w3': jax.random.uniform(ks[5], (E, H, D), jnp.float32, -sh, sh), 'expert_b3': jnp.zeros((E, D), jnp.float32)}
    _L0_ffn_all = _L0_ffn_setup()
    _L0_ffn_in = {k: v for k, v in _L0_ffn_all.items() if k in ('router_w1', 'router_b1', 'router_w2', 'router_b2', 'expert_w1', 'expert_b1', 'expert_w2', 'expert_b2', 'expert_w3', 'expert_b3')}
    del _L0_ffn_all
    return {'x': x, 'L0_tok_A_log': _L0_tok_in['A_log'], 'L0_tok_D': _L0_tok_in['D'], 'L0_tok_W_dbc': _L0_tok_in['W_dbc'], 'L0_tok_W_dt': _L0_tok_in['W_dt'], 'L0_tok_b_dt': _L0_tok_in['b_dt'], 'L0_attn_wqv_w': _L0_attn_in['wqv_w'], 'L0_attn_wqv_b': _L0_attn_in['wqv_b'], 'L0_attn_wk': _L0_attn_in['wk'], 'L0_attn_fanin_w': _L0_attn_in['fanin_w'], 'L0_attn_fanin_b': _L0_attn_in['fanin_b'], 'L0_ffn_router_w1': _L0_ffn_in['router_w1'], 'L0_ffn_router_b1': _L0_ffn_in['router_b1'], 'L0_ffn_router_w2': _L0_ffn_in['router_w2'], 'L0_ffn_router_b2': _L0_ffn_in['router_b2'], 'L0_ffn_expert_w1': _L0_ffn_in['expert_w1'], 'L0_ffn_expert_b1': _L0_ffn_in['expert_b1'], 'L0_ffn_expert_w2': _L0_ffn_in['expert_w2'], 'L0_ffn_expert_b2': _L0_ffn_in['expert_b2'], 'L0_ffn_expert_w3': _L0_ffn_in['expert_w3'], 'L0_ffn_expert_b3': _L0_ffn_in['expert_b3']}

def reference(x, L0_tok_A_log, L0_tok_D, L0_tok_W_dbc, L0_tok_W_dt, L0_tok_b_dt, L0_attn_wqv_w, L0_attn_wqv_b, L0_attn_wk, L0_attn_fanin_w, L0_attn_fanin_b, L0_ffn_router_w1, L0_ffn_router_b1, L0_ffn_router_w2, L0_ffn_router_b2, L0_ffn_expert_w1, L0_ffn_expert_b1, L0_ffn_expert_w2, L0_ffn_expert_b2, L0_ffn_expert_w3, L0_ffn_expert_b3):
    import jax
    import jax.numpy as jnp

    def _L0_tok_ref(x, A_log, D, W_dbc, W_dt, b_dt):
        import jax, jax.numpy as jnp
        import numpy as np
        BATCH = 2
        SEQ = 1024
        D_MODEL = 64
        N_STATE = 64
        DT_RANK = 1
        NUM_LAYERS = 3

        def _ssm_layer(x, A_log, Dp, W_dbc, W_dt, b_dt):
            A = -jnp.exp(A_log)
            dbc = jnp.einsum('ble,ce->blc', x, W_dbc)
            delta, Bm, Cm = jnp.split(dbc, [DT_RANK, DT_RANK + N_STATE], axis=-1)
            delta = jax.nn.softplus(jnp.einsum('blr,er->ble', delta, W_dt) + b_dt)
            dA = jnp.exp(delta[..., None] * A)
            dBx = (delta * x)[..., None] * Bm[:, :, None, :]

            def combine(c1, c2):
                a1, h1 = c1
                a2, h2 = c2
                return (a1 * a2, h1 * a2 + h2)
            _, hs = jax.lax.associative_scan(combine, (dA, dBx), axis=1)
            y = jnp.einsum('blen,bln->ble', hs, Cm)
            return y + Dp * x
        for i in range(NUM_LAYERS):
            x = _ssm_layer(x, A_log[i], D[i], W_dbc[i], W_dt[i], b_dt[i])
            if i < NUM_LAYERS - 1:
                b, l, d = x.shape
                x = x[:, :l // 2 * 2].reshape(b, l // 2, 2, d).mean(axis=2)
        return x

    def _L0_attn_ref(x, wqv_w, wqv_b, wk, fanin_w, fanin_b):
        import jax, jax.numpy as jnp
        import numpy as np
        D_MODEL = 64
        N_HEAD = 8

        def _l1_scores(q, k):
            scale = 1.0 / np.sqrt(q.shape[-1]).astype(np.float32)
            q_sbhw = q.transpose(1, 0, 2, 3)

            def one_query(qs):
                return -jnp.sum(jnp.abs(qs[:, None, :, :] - k), axis=-1) * scale
            s = jax.lax.map(one_query, q_sbhw)
            return s.transpose(1, 0, 2, 3)
        b, t, d = x.shape
        h = N_HEAD
        v = (x @ wqv_w.T + wqv_b).reshape(b, t, 3 * h, d)
        q, vf, vb = (v[:, :, :h], v[:, :, h:2 * h], v[:, :, 2 * h:])
        k = x[:, :, None, :] * wk[None, None]
        a = _l1_scores(q, k)
        a = jnp.concatenate([a, jnp.zeros((b, 1, t, h), a.dtype)], axis=1)
        a = jax.nn.softmax(a, axis=1)[:, :t]
        bf = jnp.einsum('bsdh,bshw->bdhw', a, vf)
        bb = jnp.einsum('bdsh,bshw->bdhw', a, vb)
        o = (bf + bb).sum(axis=2).reshape(b, t, d)
        y = o * jax.nn.sigmoid(1.702 * o)
        y = y @ fanin_w.T + fanin_b
        return x + y

    def _L0_ffn_ref(features, router_w1, router_b1, router_w2, router_b2, expert_w1, expert_b1, expert_w2, expert_b2, expert_w3, expert_b3):
        import jax, jax.numpy as jnp
        import numpy as np
        E, D, H, TOP_K = (6, 64, 64, 2)
        ROUTER_H = D // 2
        rh = jax.nn.relu(features @ router_w1 + router_b1)
        expert_logits = jax.nn.softmax(rh @ router_w2 + router_b2, axis=-1)
        top_w, top_i = jax.lax.top_k(expert_logits, TOP_K)
        routing_weights = jax.nn.softmax(top_w, axis=-1)
        h1 = jax.nn.relu(jnp.einsum('bsd,edh->bseh', features, expert_w1) + expert_b1)
        h2 = jax.nn.relu(jnp.einsum('bseh,ehf->bsef', h1, expert_w2) + expert_b2)
        expert_out = jnp.einsum('bsef,efo->bseo', h2, expert_w3) + expert_b3
        sel = jnp.take_along_axis(expert_out, top_i[:, :, :, None], axis=2)
        combined = jnp.sum(sel * routing_weights[..., None], axis=2)
        return combined
    h = _L0_tok_ref(x, L0_tok_A_log, L0_tok_D, L0_tok_W_dbc, L0_tok_W_dt, L0_tok_b_dt)
    h = h + _L0_attn_ref(_layernorm(h, axis=-1), L0_attn_wqv_w, L0_attn_wqv_b, L0_attn_wk, L0_attn_fanin_w, L0_attn_fanin_b)
    h = h + _L0_ffn_ref(_layernorm(h, axis=-1), L0_ffn_router_w1, L0_ffn_router_b1, L0_ffn_router_w2, L0_ffn_router_b2, L0_ffn_expert_w1, L0_ffn_expert_b1, L0_ffn_expert_w2, L0_ffn_expert_b2, L0_ffn_expert_w3, L0_ffn_expert_b3)
    return h

_drawn_inputs = setup_inputs


def setup_inputs(seed=0):
    import zlib

    import numpy as np

    out = dict(_drawn_inputs(seed))
    spreads = {'L0_tok_D': (1.0, 0.2),
     'L0_tok_b_dt': (0.0, 0.606),
     'L0_attn_wqv_b': (0.0, 2.0),
     'L0_attn_wk': (0.004999999888241291, 0.6),
     'L0_attn_fanin_b': (0.0, 0.1),
     'L0_ffn_router_b1': (0.0, 0.291),
     'L0_ffn_router_b2': (0.0, 0.1),
     'L0_ffn_expert_b1': (0.0, 0.8),
     'L0_ffn_expert_b2': (0.0, 0.43),
     'L0_ffn_expert_b3': (0.0, 0.1)}
    factors = {'L0_tok_A_log': 107.658,
     'L0_tok_W_dt': 54.13,
     'L0_attn_wqv_w': 200.0,
     'L0_attn_fanin_w': 64.0}
    for name, (base, spread) in spreads.items():
        noise = np.random.default_rng([zlib.crc32(name.encode()), seed]).standard_normal(out[name].shape)
        drawn = base * np.exp(spread * noise) if base else spread * noise
        out[name] = jnp.asarray(drawn.astype(out[name].dtype))
    for name, factor in factors.items():
        out[name] = (out[name] * factor).astype(out[name].dtype)
    return out
```

```python
import concourse.bass as bass
from concourse import mybir
from contextlib import ExitStack
import numpy as np

BATCH, SEQ, D, NS, LAYERS = 64, 125, 64, 64, 3
HB = BATCH // 2
LEN = [SEQ, SEQ // 2, SEQ // 4]
CB = [4, 8, 16]
W = [CB[l] * LEN[l] for l in range(LAYERS)]
CH = [HB // CB[l] for l in range(LAYERS)]
BASE = [0, CH[0], CH[0] + CH[1]]
NCH = sum(CH)
PAIRS = D // 2
WMAX = 512
T = LEN[2]
HALF = HB * T
COLS = HALF // 2
NHP = 4
NE = 6
TT = 4 * T
EPS = 1e-5


def build(nc, d, out):
    F = mybir.dt.float32
    BF = mybir.dt.bfloat16
    ALU = mybir.AluOpType
    ACT = mybir.ActivationFunctionType
    AX = mybir.AxisListType
    ctx = ExitStack()
    ssm = ExitStack()
    with ctx:
        def sb(name, shape, dt=F, stack=ctx):
            return stack.enter_context(nc.sbuf_tensor(name, shape, dt))

        def sem(name):
            return ctx.enter_context(nc.semaphore(name))

        h_tok = sb("h_tok", [128, HALF])
        mean_w = sb("mean_w", [128, 128])
        ident = sb("ident", [128, 128])
        w_q = sb("w_q", [128, 2, NHP, 128])
        b_q = sb("b_q", [128, NHP])
        w_k = sb("w_k", [128, NHP])
        sel_k = sb("sel_k", [128, 2, 128])
        w_v = sb("w_v", [128, 2, 4, 256])
        b_v = sb("b_v", [128, 256])
        sel_key = sb("sel_key", [128, T, 64])
        key_rows = sb("key_rows", [128, 1])
        w_fan = sb("w_fan", [128, 128])
        b_fan = sb("b_fan", [128, 1])
        w_r1 = sb("w_r1", [128, 64])
        b_r1 = sb("b_r1", [64, 1])
        w_r2 = sb("w_r2", [64, 2 * NE])
        b_r2 = sb("b_r2", [TT, NE])
        lower = sb("lower", [TT, 2, NE, NE])
        w_e1 = sb("w_e1", [128, 2, NE // 2, 128])
        b_e1 = sb("b_e1", [128, NE // 2])
        w_e2 = sb("w_e2", [128, NE // 2, 128])
        b_e2 = sb("b_e2", [128, NE // 2])
        w_e3 = sb("w_e3", [128, NE // 2, 128])
        b_e3 = sb("b_e3", [TT, NE * D])

        def sb1(name, shape, dt=F):
            return sb(name, shape, dt, ssm)

        x_l = [sb1("x_l0", [128, CH[0], W[0]]), sb1("x_l1", [128, 2 * CH[1], W[1] // 2]), sb1("x_l2", [128, 2 * CH[2], W[2] // 2])]
        w_ssm = sb1("w_ssm", [128, LAYERS, 3, 128])
        vecs = sb1("vecs", [128, LAYERS, 3])
        dskip = sb1("dskip", [128, LAYERS])
        a_neg = sb1("a_neg", [128, LAYERS, D])
        sel_red = sb1("sel_red", [128, 2, 16, 32])
        sel_bc = sb1("sel_bc", [96, 16, 128], BF)

        parts = sb1("parts", [96, 2, 4, 2, W[0]], BF)
        bmat = sb1("bmat", [128, 2, W[0]])
        cmat = sb1("cmat", [128, 2, W[0]])
        z = sb1("z", [128, W[0]])
        az = sb1("az", [128, W[0]])
        ez = sb1("ez", [128, W[0]])
        lnz = sb1("lnz", [128, W[0]])
        onepe = sb1("onepe", [128, W[0]])
        lost = sb1("lost", [128, W[0]])
        sp0 = sb1("sp0", [128, W[0]])
        src = sb1("src", [128, 2, W[0]])
        rest = sb1("rest", [128, 2, W[0]])
        hi = sb1("hi", [128, 2, W[0]], BF)
        mid = sb1("mid", [128, 2, W[0]], BF)
        lo = sb1("lo", [128, 2, W[0]], BF)
        RA, RU, RH, RG = 4, 4, 4, 4
        decay = sb1("decay", [128, RA, 2 * W[0]])
        u = sb1("u", [128, RU, 2 * W[0]])
        h = sb1("h", [128, RH, 2 * W[0]])
        g = sb1("g", [128, RG, 2 * W[0]])
        y_sb = sb1("y_sb", [128, W[0]])

        ps_delta = ssm.enter_context(nc.psum_tensor("ps_delta", [128, 2, 512], F))
        ps_dx = ssm.enter_context(nc.psum_tensor("ps_dx", [128, 2, 2, 512], F))
        ps_y = ssm.enter_context(nc.psum_tensor("ps_y", [128, 512], F))
        ps_proj = ssm.enter_context(nc.psum_tensor("ps_proj", [128, 512], F))

        ssm.close()

        normed = sb("normed", [128, HB, 32])
        h_att = sb("h_att", [128, HALF])
        res = sb("res", [128, HALF])
        cent = sb("cent", [128, HALF])
        sq = sb("sq", [128, HALF])
        rstd = sb("rstd", [128, HALF])
        scores = sb("scores", [128, 2, BATCH, 32])
        scores_t = sb("scores_t", [128, 2, BATCH, 32])
        esum = sb("esum", [128, 2, BATCH])
        qk = ExitStack()
        q_all = sb("q_all", [128, NHP, BATCH * T], F, qk)
        k_all = sb("k_all", [128, NHP, BATCH * T], F, qk)
        RD = 4
        diff = sb("diff", [128, RD, HALF], F, qk)
        dist = sb("dist", [128, RD, HALF], F, qk)
        qk.close()
        vals = ExitStack()
        v_all = sb("v_all", [128, BATCH, 2, 2, D], F, vals)
        sig = sb("sig", [128, 2, 512], F, vals)
        gated = sb("gated", [128, HB, 32], F, vals)
        vals.close()
        f_in = sb("f_in", [128, HALF])
        rh = sb("rh", [64, HALF])
        h1 = sb("h1", [128, NE // 2, 2, HALF])
        h2 = sb("h2", [128, NE // 2, 2, HALF])
        logit = sb("logit", [TT, 16, NE])
        prob = sb("prob", [TT, 16, NE])
        stat = sb("stat", [TT, 4, 16])
        beats = sb("beats", [TT, 2, 16, NE * NE])
        rank = sb("rank", [TT, 16, NE])
        gate = sb("gate", [TT, 16, NE])
        eo = sb("eo", [TT, 3, NE * D])
        mix = sb("mix", [TT, 16, D])
        fin = sb("fin", [TT, 16, D])
        P = ctx.enter_context(nc.psum_tensor("P", [128, 8, 512], F))

        x_first = sem("x_first")
        x_rest = sem("x_rest")
        w_loaded = sem("w_loaded")
        a_exp = sem("a_exp")
        const_done = sem("const_done")
        delta_bcast = sem("delta_bcast")
        dx_bcast = sem("dx_bcast")
        exp_done = sem("exp_done")
        u_done = sem("u_done")
        scan_done = sem("scan_done")
        prod_done = sem("prod_done")
        reduce_done = sem("reduce_done")
        y_sum = sem("y_sum")
        y_evac = sem("y_evac")
        decay_zero = sem("decay_zero")
        proj_done = sem("proj_done")
        proj_evac = sem("proj_evac")
        act_pre = sem("act_pre")
        dve_pre = sem("dve_pre")
        parts_loaded = sem("parts_loaded")
        stored = sem("stored")
        weights_loaded = sem("weights_loaded")
        h_ready = sem("h_ready")
        ln = {n: sem("ln_" + n) for n in ("mean", "cent", "sq", "var", "eps", "sd", "rstd", "out")}
        q_proj = sem("q_proj")
        q_ready = sem("q_ready")
        k_proj = sem("k_proj")
        k_ready = sem("k_ready")
        diff_dve = sem("diff_dve")
        diff_pool = sem("diff_pool")
        dist_done = sem("dist_done")
        dist_used = sem("dist_used")
        scores_exp = sem("scores_exp")
        pad_zero = sem("pad_zero")
        softmax = sem("softmax")
        v_proj = sem("v_proj")
        v_ready = sem("v_ready")
        o_done = sem("o_done")
        sig_done = sem("sig_done")
        gated_done = sem("gated_done")
        fan_done = sem("fan_done")
        att_done = sem("att_done")
        r1_done = sem("r1_done")
        rh_ready = sem("rh_ready")
        r2_done = sem("r2_done")
        route = sem("route")
        route_exp = sem("route_exp")
        e12_done = sem("e12_done")
        e12_relu = sem("e12_relu")
        e3_done = sem("e3_done")
        e3_used = sem("e3_used")
        mixing = sem("mixing")
        mixed = sem("mixed")
        back = sem("back")
        final = sem("final")

        LAG = 5
        PRE = 8
        NDMA = 12 * 16

        PER_ACT = 6
        PER_DVE = 7

        def wait(eng, s, v):
            if isinstance(v, int) and v <= 0:
                return
            eng.wait_ge(s, v)

        def flat(t3, l, c):
            return t3[:, c, :] if l == 0 else t3[:, :, :].rearrange("p (c two) n -> p c (two n)", two=2)[:, c, :]

        def schedule(eng, step):
            for l in range(LAYERS):
                last = CH[l] - 1
                step((l, 0, 0), None if l == 0 else (l - 1, CH[l - 1] - 1, 1), (l, 1, 1))
                if last - 1 > 2:
                    with eng.Fori(0, (last - 1) // 2) as pair:
                        c = pair * 2 + 1
                        step((l, c, 1), (l, c - 1, 0), (l, c + 1, 0))
                        step((l, c + 1, 0), (l, c, 1), (l, c + 2, 1))
                elif last > 1:
                    step((l, 1, 1), (l, 0, 0), (l, 2, 0))
                    step((l, 2, 0), (l, 1, 1), (l, 3, 1))
                step((l, last, 1), (l, last - 1, 0), (l + 1, 0, 0) if l + 1 < LAYERS else None)

        TILES = [(hg, t, s, 2 * hg + hp) for hg in range(2) for t in range(T) for s in range(2) for hp in range(2)]
        BY_POOL = [i % 3 == 2 for i in range(len(TILES))]
        made = [sum(1 for o in BY_POOL[:i + 1] if o == BY_POOL[i]) for i in range(len(TILES))]

        def wait_diff(eng, i):
            eng.wait_ge(diff_pool if BY_POOL[i] else diff_dve, made[i])

        def batches(t3, s):
            return t3[:, :, :] if s is None else t3[:, 16 * s:16 * s + 16, 0:T]

        LATER = [(mean_w, "mean_w"), (ident, "ident"), (w_q, "w_q"), (b_q, "b_q"), (w_k, "w_k"), (sel_k, "sel_k"), (w_v, "w_v"),
                 (b_v, "b_v"), (sel_key, "sel_key"), (key_rows, "key_rows"), (w_fan, "w_fan"), (b_fan, "b_fan"), (w_r1, "w_r1"),
                 (b_r1, "b_r1"), (w_r2, "w_r2"), (b_r2, "b_r2"), (lower, "lower"), (w_e1, "w_e1"), (b_e1, "b_e1"), (w_e2, "w_e2"),
                 (b_e2, "b_e2"), (w_e3, "w_e3"), (b_e3, "b_e3")]
        block = ctx.enter_context(nc.Block())

        def difference(engine, eng, i, tile):
            hg, t, s, hp = tile
            wait(eng, dist_done, i - RD + 1)
            q = q_all[:, hp, s * HALF:(s + 1) * HALF].rearrange("p (b t) -> p b t", t=T)
            k = k_all[:, hp, s * HALF:(s + 1) * HALF].rearrange("p (b t) -> p b t", t=T)[:, :, t:t + 1].broadcast_to([128, HB, T])
            return engine.tensor_tensor(out=diff[:, i % RD, :].rearrange("p (b t) -> p b t", t=T), in0=q, in1=k, op=ALU.subtract)

        @block.sync
        def _(sp):
            sp.dma_start(x_l[0][:, 0, :], d["x"][:, 0:W[0]]).then_inc(x_first, 16)
            sp.dma_start(w_ssm[:], d["w_ssm"]).then_inc(w_loaded, 16)
            sp.dma_start(vecs[:], d["vecs"]).then_inc(w_loaded, 16)
            sp.dma_start(sel_bc[:], d["sel_bc"]).then_inc(w_loaded, 16)
            sp.dma_start(a_neg[:], d["a_log"]).then_inc(w_loaded, 16)
            sp.dma_start(sel_red[:], d["sel_red"]).then_inc(w_loaded, 16)
            sp.dma_start(x_l[0][:, 1:CH[0], :], d["x"][:, W[0]:].rearrange("p (c n) -> p c n", n=W[0])).then_inc(x_rest, 16)

            for tile, name in LATER:
                sp.dma_start(tile[:], d[name]).then_inc(weights_loaded, 16)

            def load_parts(l, c, slot):
                k = BASE[l] + c
                wait(sp, dx_bcast, PAIRS * (k - 1))
                for i, (piece, s, n) in enumerate(((hi, act_pre, 5), (mid, act_pre, 6), (lo, dve_pre, 7))):
                    sp.wait_ge(s, PER_ACT * k + n if s is act_pre else PER_DVE * k + n)
                    for j in range(4):
                        sp.dma_start(parts[32 * i:32 * i + 32, slot, j, :, 0:W[l]], piece[32 * j:32 * j + 32, :, 0:W[l]])\
                          .then_inc(parts_loaded, 16)

            load_parts(0, 0, 0)

            def step(chunk, prev, nxt):
                if nxt:
                    load_parts(*nxt)
            schedule(sp, step)
            sp.wait_ge(final, 1)
            sp.dma_start(out, fin[:]).then_inc(stored, 16)
            sp.wait_ge(stored, 16)

        @block.scalar
        def _(act):
            act.wait_ge(const_done, 1)
            nc.scalar.activation(a_neg[:], a_neg[:], ACT.Exp).then_inc(a_exp, 1)

            def prelude(l, c, slot, part):
                k = BASE[l] + c
                n = W[l]
                if part == 0:
                    wait(act, u_done, PAIRS * (k - 1))
                    act.wait_ge(proj_done, 3 * k + 1)
                    nc.scalar.activation(bmat[:, slot, 0:n], ps_proj[:, 0:n], ACT.Copy).then_inc(proj_evac, 1)
                elif part == 1:
                    wait(act, prod_done, PAIRS * (k - 1))
                    act.wait_ge(proj_done, 3 * k + 2)
                    nc.scalar.activation(cmat[:, slot, 0:n], ps_proj[:, 0:n], ACT.Copy).then_inc(proj_evac, 1)
                elif part == 2:
                    wait(act, dve_pre, PER_DVE * k)
                    act.wait_ge(proj_done, 3 * k + 3)
                    nc.scalar.activation(z[:, 0:n], ps_proj[:, 0:n], ACT.Identity, bias=vecs[:, l, 1:2], scale=vecs[:, l, 0:1]).then_inc(act_pre, 1)
                elif part == 3:
                    act.wait_ge(act_pre, PER_ACT * k + 1)
                    nc.scalar.activation(az[:, 0:n], z[:, 0:n], ACT.Abs).then_inc(act_pre, 1)
                elif part == 4:
                    act.wait_ge(act_pre, PER_ACT * k + 2)
                    nc.scalar.activation(ez[:, 0:n], az[:, 0:n], ACT.Exp, scale=-1.0).then_inc(act_pre, 1)
                elif part == 5:
                    act.wait_ge(act_pre, PER_ACT * k + 3)
                    nc.scalar.activation(lnz[:, 0:n], ez[:, 0:n], ACT.Ln, bias=1.0).then_inc(act_pre, 1)
                elif part == 6:
                    wait(act, parts_loaded, NDMA * k)
                    act.wait_ge(dve_pre, PER_DVE * k + 5)
                    nc.scalar.activation(hi[:, :, 0:n], src[:, :, 0:n], ACT.Copy).then_inc(act_pre, 1)
                elif part == 7:
                    act.wait_ge(dve_pre, PER_DVE * k + 6)
                    nc.scalar.activation(mid[:, :, 0:n], rest[:, :, 0:n], ACT.Copy).then_inc(act_pre, 1)

            AT = {PRE + 1: 0, PRE + 3: 1, PRE + 5: 2, PRE + 6: 3, PRE + 7: 4, PRE + 8: 5, PRE + 11: 6, PRE + 13: 7}
            for part in range(8):
                prelude(0, 0, 0, part)

            def step(chunk, prev, nxt):
                l, c, slot = chunk
                k = BASE[l] + c
                if isinstance(c, int) and c == 0:
                    act.wait_ge(decay_zero, l + 1)
                for q in range(PAIRS):
                    G = PAIRS * k + q
                    wait(act, scan_done, G - RA + 1)
                    for r in range(2):
                        e = 16 * ((2 * q + r) % 4) + q // 2
                        act.wait_ge(delta_bcast, 2 * G + r + 1)
                        dst = decay[:, q % RA, r * W[l]:(r + 1) * W[l]].rearrange("p (b t) -> p b t", t=LEN[l])
                        s = ps_delta[:, r, 0:W[l]].rearrange("p (b t) -> p b t", t=LEN[l])
                        nc.scalar.activation(dst[:, :, 1:], s[:, :, 1:], ACT.Exp, scale=a_neg[:, l, e:e + 1]).then_inc(exp_done, 1)
                    if nxt and q in AT:
                        prelude(*nxt, AT[q])
            act.wait_ge(const_done, 2)
            schedule(act, step)
            act.wait_ge(weights_loaded, 16 * len(LATER))

            def norm(n):
                for c in range(2):
                    cols = slice(c * COLS, (c + 1) * COLS)
                    act.wait_ge(ln["cent"], 2 * n + c + 1)
                    nc.scalar.activation(sq[:, cols], cent[:, cols], ACT.Square).then_inc(ln["sq"], 1)
                for c in range(2):
                    cols = slice(c * COLS, (c + 1) * COLS)
                    act.wait_ge(ln["eps"], 2 * n + c + 1)
                    nc.scalar.activation(rstd[:, cols], rstd[:, cols], ACT.Sqrt).then_inc(ln["sd"], 1)

            norm(0)
            for i in range(16):
                hp, s, c = i // 4, i // 2 % 2, i % 2
                act.wait_ge(q_proj, i + 1)
                nc.scalar.activation(q_all[:, hp, s * HALF + c * COLS:s * HALF + (c + 1) * COLS], P[:, 4 + i % 4, 0:COLS], ACT.Identity,
                                     bias=b_q[:, hp:hp + 1]).then_inc(q_ready, 1)

            def exps(hg):
                act.wait_ge(dist_used, len(TILES) // 2 * (hg + 1))
                act.wait_ge(pad_zero, 2)
                for i in range(4):
                    s, c = i // 2, i % 2
                    nc.scalar.activation(scores[:, hg, 32 * s + 16 * c:32 * s + 16 * c + 16, 0:T],
                                         P[:, 4 * hg + i, 0:COLS].rearrange("p (b t) -> p b t", t=T), ACT.Exp, scale=-0.125).then_inc(scores_exp, 1)

            for i in range(len(TILES)):
                wait_diff(act, i)
                wait(act, dist_used, i - RD + 1)
                nc.scalar.activation(dist[:, i % RD, :], diff[:, i % RD, :], ACT.Abs).then_inc(dist_done, 1)
                if i == len(TILES) // 2 + 8:
                    exps(0)
            exps(1)
            for c in range(2):
                act.wait_ge(o_done, c + 1)
                nc.scalar.activation(sig[:, c, :], P[:, 4 + c, :], ACT.Sigmoid, scale=1.702).then_inc(sig_done, 1)
            norm(1)
            for c in range(2):
                act.wait_ge(r1_done, c + 1)
                nc.scalar.activation(rh[:, c * COLS:(c + 1) * COLS], P[0:64, 4 + c, 0:COLS], ACT.Relu, bias=b_r1[:, 0:1]).then_inc(rh_ready, 1)
            act.wait_ge(route, 3)
            nc.scalar.activation(prob[:], logit[:], ACT.Exp).then_inc(route_exp, 1)
            act.wait_ge(route, 6)
            nc.scalar.activation(gate[:], prob[:], ACT.Exp).then_inc(route_exp, 1)
            for i in range(24):
                layer, pair, s, c = i // 12, i // 4 % 3, i // 2 % 2, i % 2
                act.wait_ge(e12_done, i + 1)
                nc.scalar.activation((h2 if layer else h1)[:, pair, s, c * COLS:(c + 1) * COLS], P[:, i % 4, 0:COLS], ACT.Relu,
                                     bias=(b_e2 if layer else b_e1)[:, pair:pair + 1]).then_inc(e12_relu, 1)

        @block.vector
        def _(dve):
            dve.wait_ge(w_loaded, 80)
            nc.vector.tensor_scalar(out=a_neg[:], in0=a_neg[:], scalar1=80.0, scalar2=None, op0=ALU.min).then_inc(const_done, 1)
            dve.wait_ge(a_exp, 1)
            nc.vector.tensor_scalar(out=a_neg[:], in0=a_neg[:], scalar1=-1.0, scalar2=None, op0=ALU.mult).then_inc(const_done, 1)
            for l in range(LAYERS):
                last = nc.vector.tensor_scalar(out=dskip[:, l:l + 1], in0=vecs[:, l, 2:3], scalar1=0.5 if l < 2 else 1.0, scalar2=None, op0=ALU.mult)
            last.then_inc(const_done, 1)

            def prelude(l, c, slot, part):
                k = BASE[l] + c
                n = W[l]
                if part == 0:
                    act_ready = PER_ACT * k + 4
                    dve.wait_ge(act_pre, act_ready)
                    nc.vector.tensor_scalar(out=onepe[:, 0:n], in0=ez[:, 0:n], scalar1=1.0, scalar2=-1.0, op0=ALU.add, op1=ALU.add).then_inc(dve_pre, 1)
                    nc.vector.scalar_tensor_tensor(out=sp0[:, 0:n], in0=z[:, 0:n], scalar=0.0, in1=lnz[:, 0:n], op0=ALU.max, op1=ALU.add).then_inc(dve_pre, 1)
                elif part == 1:
                    dve.wait_ge(dve_pre, PER_DVE * k + 1)
                    nc.vector.tensor_tensor(out=lost[:, 0:n], in0=ez[:, 0:n], in1=onepe[:, 0:n], op=ALU.subtract).then_inc(dve_pre, 1)
                    dve.wait_ge(dve_pre, PER_DVE * k + 3)
                    nc.vector.tensor_tensor(out=src[:, 0, 0:n], in0=sp0[:, 0:n], in1=lost[:, 0:n], op=ALU.add).then_inc(dve_pre, 1)
                elif part == 2:
                    dve.wait_ge(dve_pre, PER_DVE * k + 4)
                    nc.vector.tensor_tensor(out=src[:, 1, 0:n], in0=src[:, 0, 0:n], in1=flat(x_l[l], l, c), op=ALU.mult).then_inc(dve_pre, 1)
                elif part == 3:
                    dve.wait_ge(act_pre, PER_ACT * k + 5)
                    nc.vector.tensor_tensor(out=rest[:, :, 0:n], in0=src[:, :, 0:n], in1=hi[:, :, 0:n], op=ALU.subtract).then_inc(dve_pre, 1)
                elif part == 4:
                    dve.wait_ge(act_pre, PER_ACT * k + 6)
                    nc.vector.tensor_tensor(out=lo[:, :, 0:n], in0=rest[:, :, 0:n], in1=mid[:, :, 0:n], op=ALU.subtract).then_inc(dve_pre, 1)

            AT = {PRE + 9: 0, PRE + 10: 1, PRE + 11: 2, PRE + 13: 3, PRE + 15: 4}
            dve.wait_ge(x_first, 16)
            for part in range(5):
                prelude(0, 0, 0, part)
            dve.wait_ge(x_rest, 16)

            def finish(l, c, slot):
                k = BASE[l] + c
                n = W[l]
                dve.wait_ge(reduce_done, PAIRS * (k + 1))
                if l < 2:
                    if not (isinstance(k, int) and k == 0):
                        dve.wait_ge(y_evac, k)
                    nc.vector.scalar_tensor_tensor(out=y_sb[:, 0:n], in0=flat(x_l[l], l, c), scalar=dskip[:, l:l + 1], in1=ps_y[:, 0:n], op0=ALU.mult, op1=ALU.add).then_inc(y_sum, 1)
                    dve.wait_ge(y_sum, k + 1)
                    pairs = y_sb[:, 0:n].rearrange("p (b t) -> p b t", t=LEN[l])[:, :, 0:2 * LEN[l + 1]].rearrange("p b (t two) -> p b t two", two=2)
                    dst = x_l[l + 1][:, c, :].rearrange("p (b t) -> p b t", t=LEN[l + 1])
                    nc.vector.tensor_tensor(out=dst, in0=pairs[:, :, :, 0], in1=pairs[:, :, :, 1], op=ALU.add).then_inc(y_evac, 1)
                else:
                    nc.vector.scalar_tensor_tensor(out=h_tok[:, c * n:(c + 1) * n], in0=flat(x_l[l], l, c), scalar=dskip[:, l:l + 1], in1=ps_y[:, 0:n], op0=ALU.mult, op1=ALU.add).then_inc(y_evac, 1)

            def inputs(l, k, slot, q):
                G = PAIRS * k + q
                dve.wait_ge(dx_bcast, G + 1)
                wait(dve, scan_done, G - RU + 1)
                nc.vector.tensor_tensor(out=u[:, q % RU, 0:2 * W[l]].rearrange("p (r n) -> p r n", r=2), in0=ps_dx[:, q % 2, :, 0:W[l]],
                                        in1=bmat[:, slot, 0:W[l]].unsqueeze(1).broadcast_to([128, 2, W[l]]), op=ALU.mult).then_inc(u_done, 1)

            def step(chunk, prev, nxt):
                l, c, slot = chunk
                k = BASE[l] + c
                if isinstance(c, int) and c == 0:
                    wait(dve, scan_done, PAIRS * k)
                    for a in range(RA):
                        dst = decay[:, a, 0:2 * W[l]].rearrange("p (b t) -> p b t", t=LEN[l])[:, :, 0:1]
                        last = nc.vector.memset(dst, 0.0)
                    last.then_inc(decay_zero, 1)
                dve.wait_ge(proj_evac, 2 * k + 1)
                inputs(l, k, slot, 0)
                for q in range(PAIRS):
                    G = PAIRS * k + q
                    if q + 1 < PAIRS:
                        inputs(l, k, slot, q + 1)
                    dve.wait_ge(u_done, G + 1)
                    dve.wait_ge(exp_done, 2 * G + 2)
                    wait(dve, prod_done, G - RH + 1)
                    nc.vector.tensor_tensor_scan(out=h[:, q % RH, 0:2 * W[l]], data0=decay[:, q % RA, 0:2 * W[l]], data1=u[:, q % RU, 0:2 * W[l]],
                                                 initial=0.0, op0=ALU.mult, op1=ALU.add).then_inc(scan_done, 1)
                    if prev and q == LAG - 1:
                        finish(*prev)
                    if nxt and q in AT:
                        prelude(*nxt, AT[q])
            dve.wait_ge(const_done, 3)
            schedule(dve, step)
            finish(LAYERS - 1, CH[-1] - 1, 1)
            dve.wait_ge(weights_loaded, 16 * len(LATER))

            def norm(n, x, dst, after):
                for c in range(2):
                    cols = slice(c * COLS, (c + 1) * COLS)
                    dve.wait_ge(ln["mean"], 2 * n + c + 1)
                    nc.vector.tensor_tensor(out=cent[:, cols], in0=x[:, cols], in1=P[:, c, 0:COLS], op=ALU.subtract).then_inc(ln["cent"], 1)
                for c in range(2):
                    cols = slice(c * COLS, (c + 1) * COLS)
                    dve.wait_ge(ln["var"], 2 * n + c + 1)
                    nc.vector.tensor_scalar(out=rstd[:, cols], in0=P[:, 2 + c, 0:COLS], scalar1=EPS, scalar2=None, op0=ALU.add).then_inc(ln["eps"], 1)
                for c in range(2):
                    cols = slice(c * COLS, (c + 1) * COLS)
                    dve.wait_ge(ln["sd"], 2 * n + c + 1)
                    nc.vector.reciprocal(sq[:, cols], rstd[:, cols]).then_inc(ln["rstd"], 1)
                    dve.wait_ge(ln["rstd"], 2 * n + c + 1)
                    nc.vector.tensor_tensor(out=dst(c), in0=cent[:, cols].rearrange("p (b t) -> p b t", t=T),
                                            in1=sq[:, cols].rearrange("p (b t) -> p b t", t=T), op=ALU.mult).then_inc(ln["out"], 1)

            dve.wait_ge(y_evac, NCH)
            dve.wait_ge(reduce_done, PAIRS * NCH)
            nc.vector.memset(normed[:, :, T:32], 0.0).then_inc(pad_zero, 1)
            nc.vector.memset(scores[:, :, :, T:32], 0.0).then_inc(pad_zero, 1)
            norm(0, h_tok, lambda c: normed[:, 16 * c:16 * c + 16, 0:T], 0)
            dve.wait_ge(ln["out"], 2)
            nc.vector.tensor_tensor(out=res[:, :].rearrange("p (b t) -> p b t", t=T), in0=h_tok[:, :].rearrange("p (b t) -> p b t", t=T),
                                    in1=normed[:, :, 0:T], op=ALU.add).then_inc(h_ready, 1)
            for hp in range(NHP):
                for i in range(4):
                    dve.wait_ge(k_proj, i + 1)
                    nc.vector.tensor_scalar(out=k_all[:, hp, i * COLS:(i + 1) * COLS], in0=P[:, i, 0:COLS], scalar1=w_k[:, hp:hp + 1], scalar2=None,
                                            op0=ALU.mult).then_inc(k_ready, 1)
            dve.wait_ge(k_ready, 16)
            dve.wait_ge(q_ready, 16)

            def soft(hg):
                dve.wait_ge(scores_exp, 4 * (hg + 1))
                sc = scores[:, hg, :, :]
                nc.vector.reduce_sum(esum[:, hg, :], sc, AX.X).then_inc(softmax, 1)
                dve.wait_ge(softmax, 6 * hg + 1)
                nc.vector.tensor_scalar(out=esum[:, hg, :], in0=esum[:, hg, :], scalar1=1.0, scalar2=None, op0=ALU.add).then_inc(softmax, 1)
                dve.wait_ge(softmax, 6 * hg + 2)
                nc.vector.reciprocal(esum[:, hg, :], esum[:, hg, :]).then_inc(softmax, 1)
                dve.wait_ge(softmax, 6 * hg + 3)
                nc.vector.tensor_scalar(out=esum[:, hg, :], in0=esum[:, hg, :], scalar1=key_rows[:, 0:1], scalar2=None, op0=ALU.mult).then_inc(softmax, 1)
                dve.wait_ge(softmax, 6 * hg + 4)
                nc.vector.tensor_tensor(out=sc, in0=sc, in1=esum[:, hg, :].unsqueeze(2).broadcast_to([128, BATCH, 32]), op=ALU.mult).then_inc(softmax, 1)
                dve.wait_ge(softmax, 6 * hg + 5)
                nc.vector.transpose(scores_t[:, hg, :, :].rearrange("p b t -> p (b t)"), sc.rearrange("p b t -> p (b t)")).then_inc(softmax, 1)

            for i, tile in enumerate(TILES):
                if not BY_POOL[i]:
                    difference(nc.vector, dve, i, tile).then_inc(diff_dve, 1)
                if i == len(TILES) // 2 + 24:
                    soft(0)
            soft(1)
            for i in range(32):
                dve.wait_ge(v_proj, i + 1)
                nc.vector.tensor_tensor(out=v_all[:, 2 * i:2 * i + 2, :, :, :].rearrange("p b f g w -> p b (f g w)"), in0=P[:, i % 4, :].rearrange("p (b n) -> p b n", b=2),
                                        in1=b_v[:, :].unsqueeze(1).broadcast_to([128, 2, 256]), op=ALU.add).then_inc(v_ready, 1)
            for c in range(2):
                dve.wait_ge(sig_done, c + 1)
                nc.vector.tensor_tensor(out=gated[:, 16 * c:16 * c + 16, :].rearrange("p b t -> p (b t)"), in0=P[:, 4 + c, :], in1=sig[:, c, :], op=ALU.mult).then_inc(gated_done, 1)
            dve.wait_ge(h_ready, 1)
            for c in range(2):
                cols = slice(c * COLS, (c + 1) * COLS)
                dve.wait_ge(fan_done, c + 1)
                nc.vector.scalar_tensor_tensor(out=h_att[:, cols], in0=P[:, 6 + c, 0:COLS], scalar=b_fan[:, 0:1], in1=res[:, cols], op0=ALU.add, op1=ALU.add).then_inc(att_done, 1)
            dve.wait_ge(att_done, 2)
            norm(1, h_att, lambda c: f_in[:, c * COLS:(c + 1) * COLS].rearrange("p (b t) -> p b t", t=T), 0)

            link = [0]

            def chained(ins):
                link[0] += 1
                ins.then_inc(route, 1)
                dve.wait_ge(route, link[0])

            def per_expert(v):
                return v.unsqueeze(2).broadcast_to([TT, 16, NE])

            dve.wait_ge(r2_done, 1)
            chained(nc.vector.tensor_tensor(out=logit[:], in0=P[0:TT, 7, 0:96].rearrange("p (k e) -> p k e", e=NE),
                                            in1=b_r2[:, :].unsqueeze(1).broadcast_to([TT, 16, NE]), op=ALU.add))
            chained(nc.vector.reduce_max(stat[:, 0, :], logit[:], AX.X))
            chained(nc.vector.tensor_tensor(out=logit[:], in0=logit[:], in1=per_expert(stat[:, 0, :]), op=ALU.subtract))
            dve.wait_ge(route_exp, 1)
            chained(nc.vector.reduce_sum(stat[:, 1, :], prob[:], AX.X))
            chained(nc.vector.reciprocal(stat[:, 2, :], stat[:, 1, :]))
            chained(nc.vector.tensor_tensor(out=prob[:], in0=prob[:], in1=per_expert(stat[:, 2, :]), op=ALU.mult))
            for n, op in ((0, ALU.is_ge), (1, ALU.is_gt)):
                for e in range(NE):
                    chained(nc.vector.tensor_tensor(out=beats[:, n, :, e * NE:(e + 1) * NE], in0=prob[:], in1=prob[:, :, e:e + 1].broadcast_to([TT, 16, NE]), op=op))
                chained(nc.vector.tensor_tensor(out=beats[:, n, :, :], in0=beats[:, n, :, :], in1=lower[:, n, :, :].rearrange("p a b -> p (a b)").unsqueeze(1).broadcast_to([TT, 16, NE * NE]), op=ALU.mult))
            chained(nc.vector.tensor_tensor(out=beats[:, 0, :, :], in0=beats[:, 0, :, :], in1=beats[:, 1, :, :], op=ALU.add))
            chained(nc.vector.reduce_sum(rank[:].rearrange("p k e -> p (k e)"), beats[:, 0, :, :].rearrange("p k (i j) -> p (k i) j", j=NE), AX.X))
            chained(nc.vector.tensor_scalar(out=rank[:], in0=rank[:], scalar1=2.0, scalar2=None, op0=ALU.is_lt))
            dve.wait_ge(route_exp, 2)
            chained(nc.vector.tensor_tensor(out=gate[:], in0=gate[:], in1=rank[:], op=ALU.mult))
            chained(nc.vector.reduce_sum(stat[:, 3, :], gate[:], AX.X))
            chained(nc.vector.reciprocal(stat[:, 0, :], stat[:, 3, :]))
            chained(nc.vector.tensor_tensor(out=gate[:], in0=gate[:], in1=per_expert(stat[:, 0, :]), op=ALU.mult))

            def experts(v):
                return v.rearrange("p (e o) -> p e o", e=NE)

            def weigh(i):
                dve.wait_ge(e3_used, i + 1)
                nc.vector.tensor_tensor(out=experts(eo[:, i % 3, :]), in0=experts(eo[:, i % 3, :]), in1=gate[:, i, :].unsqueeze(2).broadcast_to([TT, NE, D]),
                                        op=ALU.mult).then_inc(mixing, 1)

            def collect(i):
                dve.wait_ge(mixing, i + 1)
                nc.vector.reduce_sum(mix[:, i, :], eo[:, i % 3, :].rearrange("p (e o) -> p o e", e=NE), AX.X).then_inc(mixed, 1)

            for i in range(16):
                dve.wait_ge(e3_done, i + 1)
                wait(dve, mixed, i - 2)
                nc.vector.tensor_tensor(out=eo[:, i % 3, :], in0=P[0:TT, 4 + i % 3, 0:NE * D], in1=b_e3[:], op=ALU.add).then_inc(e3_used, 1)
                if i:
                    weigh(i - 1)
                if i > 1:
                    collect(i - 2)
            weigh(15)
            collect(14)
            collect(15)
            dve.wait_ge(back, 8)
            dve.wait_ge(mixed, 16)
            for c in range(2):
                for s in range(2):
                    def tiles(t3):
                        return t3[:, 8 * c:8 * c + 8, :].rearrange("p (k s) (j l) -> p s k j l", s=2, j=4)[:, s, :, :, :]
                    last = nc.vector.tensor_tensor(out=tiles(fin), in0=tiles(mix), in1=P[0:TT, c, :].rearrange("p (k j s l) -> p s k j l", k=4, j=4, s=2)[:, s, :, :, :], op=ALU.add)
            last.then_inc(final, 1)

        @block.gpsimd
        def _(pool):
            def step(chunk, prev, nxt):
                l, c, slot = chunk
                k = BASE[l] + c
                pool.wait_ge(proj_evac, 2 * k + 2)
                for q in range(PAIRS):
                    G = PAIRS * k + q
                    pool.wait_ge(scan_done, G + 1)
                    wait(pool, reduce_done, G - RG + 1)
                    nc.gpsimd.tensor_tensor(out=g[:, q % RG, 0:2 * W[l]].rearrange("p (r n) -> p r n", r=2),
                                            in0=h[:, q % RH, 0:2 * W[l]].rearrange("p (r n) -> p r n", r=2),
                                            in1=cmat[:, slot, 0:W[l]].unsqueeze(1).broadcast_to([128, 2, W[l]]), op=ALU.mult).then_inc(prod_done, 1)
            schedule(pool, step)
            pool.wait_ge(k_ready, 16)
            pool.wait_ge(q_ready, 16)
            for i, tile in enumerate(TILES):
                if BY_POOL[i]:
                    difference(nc.gpsimd, pool, i, tile).then_inc(diff_pool, 1)

        @block.tensor
        def _(pe):
            pe.wait_ge(w_loaded, 80)
            pe.wait_ge(x_first, 16)

            def project(l, c, slot, part):
                k = BASE[l] + c
                if l > 0:
                    pe.wait_ge(y_evac, BASE[l - 1] + 2 * c + 2)
                if part == 0:
                    wait(pe, act_pre, PER_ACT * (k - 1) + 1)
                else:
                    pe.wait_ge(proj_evac, 2 * k + part)
                nc.tensor.matmul(ps_proj[:, 0:W[l]], w_ssm[:, l, part, :], flat(x_l[l], l, c), start=True, stop=True).then_inc(proj_done, 1)

            for part in range(3):
                project(0, 0, 0, part)
            pe.wait_ge(x_rest, 16)

            def reduce(l, c, slot, q):
                G = PAIRS * (BASE[l] + c) + q
                pe.wait_ge(prod_done, G + 1)
                if q == 0:
                    wait(pe, y_evac, BASE[l] + c)
                for r in range(2):
                    j = (2 * q + r) % 4
                    el = q // 2
                    last = nc.tensor.matmul(ps_y[32 * j:32 * j + 32, 0:W[l]], sel_red[:, 0 if l < 2 else 1, el, :], g[:, q % RG, r * W[l]:(r + 1) * W[l]],
                                            start=(el == 0), stop=(el == 15), tile_position=(0, 32 * j))
                last.then_inc(reduce_done, 1)

            AT = {PRE: 0, PRE + 2: 1, PRE + 4: 2}

            def step(chunk, prev, nxt):
                l, c, slot = chunk
                k = BASE[l] + c
                pe.wait_ge(parts_loaded, NDMA * (k + 1))
                for q in range(PAIRS):
                    G = PAIRS * k + q
                    el = q // 2
                    for r in range(2):
                        j = (2 * q + r) % 4
                        wait(pe, exp_done, 2 * G + r - 1)
                        nc.tensor.matmul(ps_delta[:, r, 0:W[l]], sel_bc[:, el, :], parts[:, slot, j, 0, 0:W[l]], start=True, stop=True).then_inc(delta_bcast, 1)
                    wait(pe, u_done, G - 1)
                    for r in range(2):
                        j = (2 * q + r) % 4
                        last = nc.tensor.matmul(ps_dx[:, q % 2, r, 0:W[l]], sel_bc[:, el, :], parts[:, slot, j, 1, 0:W[l]], start=True, stop=True)
                    last.then_inc(dx_bcast, 1)
                    if q >= LAG:
                        reduce(l, c, slot, q - LAG)
                    elif prev:
                        reduce(*prev, PAIRS - LAG + q)
                    if nxt and q in AT:
                        project(*nxt, AT[q])
            schedule(pe, step)
            for q in range(PAIRS - LAG, PAIRS):
                reduce(LAYERS - 1, CH[-1] - 1, 1, q)
            pe.wait_ge(weights_loaded, 16 * len(LATER))

            def norm(n, x, ready, count):
                for c in range(2):
                    pe.wait_ge(ready, count)
                    nc.tensor.matmul(P[:, c, 0:COLS], mean_w[:], x[:, c * COLS:(c + 1) * COLS], start=True, stop=True).then_inc(ln["mean"], 1)
                for c in range(2):
                    pe.wait_ge(ln["sq"], 2 * n + c + 1)
                    nc.tensor.matmul(P[:, 2 + c, 0:COLS], mean_w[:], sq[:, c * COLS:(c + 1) * COLS], start=True, stop=True).then_inc(ln["var"], 1)

            norm(0, h_tok, y_evac, NCH)
            pe.wait_ge(ln["out"], 2)
            for i in range(4):
                s, c = i // 2, i % 2
                nc.tensor.matmul(P[:, i, 0:COLS], sel_k[:, s, :], normed[:, 16 * c:16 * c + 16, 0:T], start=True, stop=True).then_inc(k_proj, 1)
            for i in range(16):
                hp, s, c = i // 4, i // 2 % 2, i % 2
                wait(pe, q_ready, i - 3)
                nc.tensor.matmul(P[:, 4 + i % 4, 0:COLS], w_q[:, s, hp, :], normed[:, 16 * c:16 * c + 16, 0:T], start=True, stop=True).then_inc(q_proj, 1)
            pe.wait_ge(k_ready, 16)
            for i, (hg, t, s, hp) in enumerate(TILES):
                if i == len(TILES) // 2:
                    pe.wait_ge(q_ready, 16)
                pe.wait_ge(dist_done, i + 1)
                lo_row = 64 * (hp % 2)
                for c in range(2):
                    last = nc.tensor.matmul(P[lo_row:lo_row + 64, 4 * hg + 2 * s + c, 0:COLS], sel_key[:, t, :], dist[:, i % RD, c * COLS:(c + 1) * COLS],
                                            start=(t == 0), stop=(t == T - 1), tile_position=(0, lo_row))
                last.then_inc(dist_used, 1)
            pe.wait_ge(pad_zero, 1)
            pe.wait_ge(scores_exp, 4)
            for i in range(32):
                wait(pe, v_ready, i - 3)
                for b in (2 * i, 2 * i + 1):
                    for h4 in range(4):
                        last = nc.tensor.matmul(P[32 * h4:32 * h4 + 32, i % 4, 256 * (b % 2):256 * (b % 2) + 256], normed[:, b % HB, :], w_v[:, b // HB, h4, :],
                                                start=True, stop=True, tile_position=(0, 32 * h4))
                last.then_inc(v_proj, 1)
            pe.wait_ge(softmax, 12)
            pe.wait_ge(scores_exp, 8)
            pe.wait_ge(v_ready, 32)
            for b32 in range(HB):
                for s in range(2):
                    b = s * HB + b32
                    for n, (f, hg) in enumerate(((0, 0), (0, 1), (1, 0), (1, 1))):
                        last = nc.tensor.matmul(P[64 * s:64 * s + 64, 4 + b32 // 16, 32 * (b32 % 16):32 * (b32 % 16) + 32], v_all[:, b, f, hg, :],
                                                (scores if f else scores_t)[:, hg, b, :], start=(n == 0), stop=(n == 3), tile_position=(0, 64 * s))
                if b32 % 16 == 15:
                    last.then_inc(o_done, 1)
            for c in range(2):
                pe.wait_ge(gated_done, c + 1)
                nc.tensor.matmul(P[:, 6 + c, 0:COLS], w_fan[:], gated[:, 16 * c:16 * c + 16, 0:T], start=True, stop=True).then_inc(fan_done, 1)
            norm(1, h_att, att_done, 2)
            pe.wait_ge(ln["out"], 4)
            for c in range(2):
                nc.tensor.matmul(P[0:64, 4 + c, 0:COLS], w_r1[:], f_in[:, c * COLS:(c + 1) * COLS], start=True, stop=True).then_inc(r1_done, 1)
            pe.wait_ge(rh_ready, 2)
            for k in range(8):
                last = nc.tensor.matmul(P[0:TT, 7, 2 * NE * k:2 * NE * (k + 1)], rh[:, TT * k:TT * (k + 1)], w_r2[:], start=True, stop=True)
            last.then_inc(r2_done, 1)
            for i in range(24):
                layer, pair, s, c = i // 12, i // 4 % 3, i // 2 % 2, i % 2
                cols = slice(c * COLS, (c + 1) * COLS)
                wait(pe, e12_relu, max(i - 3, i - 11 if layer else 0))
                nc.tensor.matmul(P[:, i % 4, 0:COLS], w_e2[:, pair, :] if layer else w_e1[:, s, pair, :], h1[:, pair, s, cols] if layer else f_in[:, cols],
                                 start=True, stop=True).then_inc(e12_done, 1)
            pe.wait_ge(e12_relu, 24)
            for i in range(16):
                k, s = i // 2, i % 2
                wait(pe, e3_used, i - 2)
                for pair in range(NE // 2):
                    last = nc.tensor.matmul(P[0:TT, 4 + i % 3, 128 * pair:128 * pair + 128], h2[:, pair, s, TT * k:TT * (k + 1)], w_e3[:, pair, :], start=True, stop=True)
                last.then_inc(e3_done, 1)
            for k in range(8):
                nc.tensor.transpose(P[0:TT, k // 4, 128 * (k % 4):128 * (k % 4) + 128], h_att[:, TT * k:TT * (k + 1)], ident[:]).then_inc(back, 1)


def lay_out(i):
    f = np.float32
    e = np.arange(D)
    def chan(a):
        a = np.asarray(a)
        return np.repeat(a.reshape(4, 1, 16, *a.shape[1:]), 2, axis=1).reshape(128, *a.shape[1:])
    half_of = np.repeat(np.tile(np.arange(2), 4), 16)
    o = {}
    x = np.asarray(i["x"]).reshape(2, HB, SEQ, 4, 16)
    o["x"] = np.ascontiguousarray(x.transpose(3, 0, 4, 1, 2).reshape(128, HB * SEQ))
    w = np.zeros((128, LAYERS, 3, 128), f)
    for l in range(LAYERS):
        wd = np.asarray(i["L0_tok_W_dbc"][l])
        for s in range(2):
            rows = half_of == s
            for part, block in ((0, wd[1:65]), (1, wd[65:129])):
                w[rows, l, part, 64 * s:64 * s + 64] = chan(block.T)[rows]
            w[np.ix_(rows, [l], [2], rows)] = chan(wd[0])[rows][:, None, None, None]
    o["w_ssm"] = w
    v = np.zeros((128, LAYERS, 3), f)
    for l in range(LAYERS):
        v[:, l, 0] = chan(i["L0_tok_W_dt"][l][:, 0])
        v[:, l, 1] = chan(i["L0_tok_b_dt"][l])
        v[:, l, 2] = chan(i["L0_tok_D"][l])
    o["vecs"] = v
    al = np.asarray(i["L0_tok_A_log"]).transpose(2, 0, 1)
    o["a_log"] = np.concatenate([al, al], axis=0)
    wq = np.asarray(i["L0_attn_wqv_w"]).reshape(3, 4, 2, D, D)
    o["w_q"] = np.zeros((128, 2, NHP, 128), f)
    o["w_v"] = np.zeros((128, 2, 4, 2, 2, D), f)
    wv = np.asarray(i["L0_attn_wqv_w"]).reshape(3, 2, 4, D, D)[1:]
    o["w_e1"] = np.zeros((128, 2, NE // 2, 128), f)
    o["w_r1"] = np.zeros((128, 2, 32), f)
    o["w_fan"] = np.zeros((2, D, 128), f)
    for s in range(2):
        rows = half_of == s
        o["w_q"][rows, s] = chan(wq[0].transpose(3, 0, 1, 2).reshape(D, NHP, 128))[rows]
        o["w_v"][rows, s] = chan(wv.transpose(4, 2, 0, 1, 3))[rows]
        o["w_e1"][rows, s] = chan(np.asarray(i["L0_ffn_expert_w1"]).transpose(1, 0, 2).reshape(D, NE // 2, 128))[rows]
        o["w_r1"][rows, s] = chan(i["L0_ffn_router_w1"])[rows]
        o["w_fan"][s][:, rows] = chan(i["L0_attn_fanin_w"])[rows].T
    o["w_v"] = o["w_v"].reshape(128, 2, 4, 256)
    o["w_r1"] = o["w_r1"].reshape(128, 64)
    o["w_fan"] = o["w_fan"].reshape(128, 128)
    bq = np.asarray(i["L0_attn_wqv_b"]).reshape(3, 4, 128)
    o["b_q"] = bq[0].T
    o["w_k"] = np.asarray(i["L0_attn_wk"]).reshape(4, 128).T
    bv = np.asarray(i["L0_attn_wqv_b"]).reshape(3, 2, 4, 1, D)[1:].transpose(2, 3, 0, 1, 4)
    o["b_v"] = np.broadcast_to(bv, (4, 32, 2, 2, D)).reshape(128, 256)
    o["b_fan"] = chan(i["L0_attn_fanin_b"])[:, None]
    o["b_r1"] = np.tile(np.asarray(i["L0_ffn_router_b1"]), 2)[:, None]
    o["w_r2"] = np.zeros((2, 32, 2, NE), f)
    for s in range(2):
        o["w_r2"][s, :, s] = i["L0_ffn_router_w2"]
    o["w_r2"] = o["w_r2"].reshape(64, 2 * NE)
    o["b_r2"] = np.broadcast_to(np.asarray(i["L0_ffn_router_b2"]), (TT, NE))
    for n in (2, 3):
        w = np.zeros((2, D, NE // 2, 2, D), f)
        for e in range(NE):
            w[e % 2, :, e // 2, e % 2] = i[f"L0_ffn_expert_w{n}"][e]
        o[f"w_e{n}"] = w.reshape(128, NE // 2, 128)
    for n in (1, 2):
        o[f"b_e{n}"] = np.asarray(i[f"L0_ffn_expert_b{n}"]).reshape(NE // 2, 128).T
    o["b_e3"] = np.broadcast_to(np.asarray(i["L0_ffn_expert_b3"]).reshape(1, NE * D), (TT, NE * D))
    return o


def constants():
    f = np.float32
    o = {}
    s = np.zeros((2, 64, 2, 16, 2, 16), f)
    for h in range(2):
        for el in range(16):
            s[h, :, 0, el, h, el] = 0.5
            s[h, :, 1, el, h, el] = 1.0
    o["sel_red"] = s.reshape(128, 2, 16, 32)
    b = np.zeros((3, 2, 16, 16, 2, 64), f)
    for h in range(2):
        for el in range(16):
            b[:, h, el, el, h, :] = 1.0
    o["sel_bc"] = b.reshape(96, 16, 128).astype(np.dtype("bfloat16"))
    half_of = np.repeat(np.tile(np.arange(2), 4), 16)
    chan_of = (np.arange(4)[:, None, None] * 16 + np.zeros((1, 2, 1), int) + np.arange(16)).reshape(128)
    o["mean_w"] = ((half_of[:, None] == half_of[None, :]) / D).astype(f)
    o["ident"] = np.eye(128, dtype=f)
    o["sel_k"] = np.stack([((half_of == s)[:, None] & (chan_of[:, None] == np.tile(np.arange(D), 2)[None, :])) for s in range(2)], axis=1).astype(f)
    k = np.zeros((2, D, T, 2, 32), f)
    for h in range(2):
        for t in range(T):
            k[h, :, t, h, t] = 1.0
    o["sel_key"] = k.reshape(128, T, 64)
    o["key_rows"] = (np.arange(128) % 32 < T).astype(f)[:, None]
    own, other = np.meshgrid(np.arange(NE), np.arange(NE), indexing="ij")
    o["lower"] = np.broadcast_to(np.stack([other < own, other > own]).astype(f), (TT, 2, NE, NE))
    return o


def kernel(**inputs):
    import concourse.bacc as _bacc
    from concourse import mybir as _mybir
    from concourse.bass_utils import run_bass_kernel_spmd as _run
    nc = _bacc.Bacc("TRN2", target_bir_lowering=False, num_devices=1)
    arrays = {k: np.ascontiguousarray(v) for k, v in {**lay_out(inputs), **constants()}.items()}
    d = {k: nc.dram_tensor("in_" + k, a.shape, _mybir.dt.from_np(a.dtype), kind="ExternalInput").ap() for k, a in arrays.items()}
    out = nc.dram_tensor("out", (TT, 16, D), _mybir.dt.float32, kind="ExternalOutput").ap()
    build(nc, d, out)
    r = _run(nc, [{"in_" + k: a for k, a in arrays.items()}], core_ids=[0])
    o = r.results[0]["out"].reshape(4, T, 8, 2, D)
    return np.ascontiguousarray(o.transpose(3, 2, 0, 1, 4).reshape(BATCH, T, D))
```

```python
import concourse.bass as bass
from concourse import mybir
from contextlib import ExitStack
import numpy as np

BATCH, SEQ, D, NS, LAYERS = 64, 125, 64, 64, 3
HB = BATCH // 2
LEN = [SEQ // 4 * 4, SEQ // 4 * 2, SEQ // 4]
CB = [4, 8, 16]
W = CB[0] * LEN[0]
assert all(CB[l] * LEN[l] == W for l in range(LAYERS)) and SEQ // 2 // 2 == SEQ // 4
CH = [HB // CB[l] for l in range(LAYERS)]
BASE = [0, CH[0], CH[0] + CH[1]]
NCH = sum(CH)
PAIRS = D // 2
T = LEN[2]
HALF = HB * T
COLS = HALF // 2
NHP = 4
NE = 6
TT = 4 * T
EPS = 1e-5


def build(nc, d, out):
    F = mybir.dt.float32
    BF = mybir.dt.bfloat16
    ALU = mybir.AluOpType
    U32 = mybir.dt.uint32
    ACT = mybir.ActivationFunctionType
    AX = mybir.AxisListType
    ctx = ExitStack()
    ssm = ExitStack()
    with ctx:
        def sb(name, shape, dt=F, stack=ctx):
            return stack.enter_context(nc.sbuf_tensor(name, shape, dt))

        def sem(name):
            return ctx.enter_context(nc.semaphore(name))

        h_tok = sb("h_tok", [128, HALF])
        mean_w = sb("mean_w", [128, 128])
        ident = sb("ident", [128, 128])
        w_q = sb("w_q", [128, 2, NHP, 128])
        b_q = sb("b_q", [128, NHP])
        w_k = sb("w_k", [128, NHP])
        sel_k = sb("sel_k", [128, 2, 128])
        b_v = sb("b_v", [128, 256])
        sel_key = sb("sel_key", [128, T, 64])
        key_rows = sb("key_rows", [128, 1])
        w_fan = sb("w_fan", [128, 128])
        b_fan = sb("b_fan", [128, 1])
        w_r1 = sb("w_r1", [128, 64])
        b_r1 = sb("b_r1", [64, 1])
        w_r2 = sb("w_r2", [64, 2 * NE])
        b_r2 = sb("b_r2", [TT, NE])
        lower = sb("lower", [TT, 2, NE, NE])
        w_e1 = sb("w_e1", [128, 2, NE // 2, 128])
        b_e1 = sb("b_e1", [128, NE // 2])
        w_e2 = sb("w_e2", [128, NE // 2, 128])
        b_e2 = sb("b_e2", [128, NE // 2])
        w_e3 = sb("w_e3", [128, NE // 2, 128])
        b_e3 = sb("b_e3", [TT, NE * D])

        def sb1(name, shape, dt=F):
            return sb(name, shape, dt, ssm)

        x_l = [sb1("x_l0", [128, CH[0], W]), sb1("x_l1", [128, 2 * CH[1], W // 2]), sb1("x_l2", [128, 2 * CH[2], W // 2])]
        w_ssm = sb1("w_ssm", [128, LAYERS, 3, 128])
        vecs = sb1("vecs", [128, LAYERS, 2])
        a_neg = sb1("a_neg", [128, LAYERS, D])
        sel_red = sb1("sel_red", [128, 16, 32])
        sel_bc = sb1("sel_bc", [96, 16, 128], BF)

        parts = sb1("parts", [96, 2, 4, 2, W], BF)
        bmat = sb1("bmat", [128, 2, W])
        cmat = sb1("cmat", [128, 2, W])
        z = sb1("z", [128, W])
        ez = sb1("ez", [128, W])
        az = ez
        lnz = sb1("lnz", [128, W])
        onepe = sb1("onepe", [128, W])
        lost = onepe
        skip_w = sb1("skip_w", [128, LAYERS, 128])
        neg_id = sb1("neg_id", [128, 128], BF)
        sp0 = sb1("sp0", [128, W])
        src = sb1("src", [128, 2, W])
        hi = sb1("hi", [128, 2, W], BF)
        mid = sb1("mid", [128, 2, W], BF)
        lo = sb1("lo", [128, 2, W], BF)
        RA, RH, RG = 8, 8, 8
        decay = sb1("decay", [128, RA, 2 * W])
        h = sb1("h", [128, RH, 2 * W])
        g = sb1("g", [128, RG, 2 * W])
        y_sb = sb1("y_sb", [128, W])

        ps_delta = ssm.enter_context(nc.psum_tensor("ps_delta", [128, 2, 512], F))
        ps_dx = ssm.enter_context(nc.psum_tensor("ps_dx", [128, 2, 2, 512], F))
        ps_y = ssm.enter_context(nc.psum_tensor("ps_y", [128, 512], F))
        ps_proj = ssm.enter_context(nc.psum_tensor("ps_proj", [128, 512], F))

        ssm.close()

        w_v = sb("w_v", [128, 2, 4, 256])
        normed = sb("normed", [128, HB, 32])
        h_att = sb("h_att", [128, HALF])
        res = sb("res", [128, HALF])
        cent = sb("cent", [128, HALF])
        sq = sb("sq", [128, HALF])
        rstd = sb("rstd", [128, HALF])
        scores = sb("scores", [128, 2, BATCH, 32])
        scores_t = sb("scores_t", [128, 2, BATCH, 32])
        esum = sb("esum", [128, 2, BATCH])
        qk = ExitStack()
        q_all = sb("q_all", [128, NHP, BATCH * T], F, qk)
        k_all = sb("k_all", [128, NHP, BATCH * T], F, qk)
        RD = 4
        diff = sb("diff", [128, RD, HALF], F, qk)
        dist = sb("dist", [128, RD, HALF], F, qk)
        qk.close()
        vals = ExitStack()
        v_all = sb("v_all", [128, BATCH, 2, 2, D], F, vals)
        sig = sb("sig", [128, 2, 512], F, vals)
        gated = sb("gated", [128, HB, 32], F, vals)
        vals.close()
        f_in = sb("f_in", [128, HALF])
        rh = sb("rh", [64, HALF])
        h1 = sb("h1", [128, NE // 2, 2, HALF])
        h2 = sb("h2", [128, NE // 2, 2, HALF])
        logit = sb("logit", [TT, 16, NE])
        prob = sb("prob", [TT, 16, NE])
        stat = sb("stat", [TT, 4, 16])
        beats = sb("beats", [TT, 2, 16, NE * NE])
        rank = sb("rank", [TT, 16, NE])
        gate = sb("gate", [TT, 16, NE])
        eo = sb("eo", [TT, 3, NE * D])
        mix = sb("mix", [TT, 16, D])
        fin = sb("fin", [TT, 16, D])
        P = ctx.enter_context(nc.psum_tensor("P", [128, 8, 512], F))

        x_first = sem("x_first")
        x_rest = sem("x_rest")
        w_loaded = sem("w_loaded")
        a_exp = sem("a_exp")
        const_done = sem("const_done")
        delta_bcast = sem("delta_bcast")
        dx_bcast = sem("dx_bcast")
        exp_done = sem("exp_done")
        u_done = sem("u_done")
        scan_done = sem("scan_done")
        prod_done = sem("prod_done")
        reduce_done = sem("reduce_done")
        y_copy = sem("y_copy")
        pooled = sem("pooled")
        split_done = sem("split_done")
        decay_zero = sem("decay_zero")
        proj_done = sem("proj_done")
        proj_evac = sem("proj_evac")
        act_pre = sem("act_pre")
        dve_pre = sem("dve_pre")
        parts_loaded = sem("parts_loaded")
        stored = sem("stored")
        weights_loaded = sem("weights_loaded")
        w_v_loaded = sem("w_v_loaded")
        h_ready = sem("h_ready")
        ln = {n: sem("ln_" + n) for n in ("mean", "cent", "sq", "var", "eps", "sd", "rstd", "out")}
        q_proj = sem("q_proj")
        q_ready = sem("q_ready")
        k_proj = sem("k_proj")
        k_ready = sem("k_ready")
        diff_dve = sem("diff_dve")
        diff_pool = sem("diff_pool")
        dist_act = sem("dist_act")
        dist_dve = sem("dist_dve")
        dist_used = sem("dist_used")
        scores_exp = sem("scores_exp")
        pad_zero = sem("pad_zero")
        softmax = sem("softmax")
        v_proj = sem("v_proj")
        v_ready = sem("v_ready")
        o_done = sem("o_done")
        sig_done = sem("sig_done")
        gated_done = sem("gated_done")
        fan_done = sem("fan_done")
        att_done = sem("att_done")
        r1_done = sem("r1_done")
        rh_ready = sem("rh_ready")
        r2_done = sem("r2_done")
        route = sem("route")
        route_exp = sem("route_exp")
        e12_done = sem("e12_done")
        e12_relu = sem("e12_relu")
        e3_done = sem("e3_done")
        e3_used = sem("e3_used")
        mixing = sem("mixing")
        mixed = sem("mixed")
        back = sem("back")
        final = sem("final")

        LAG = 7
        PRE = 9
        NDMA = 12 * 16

        A_Z, A_AZ, A_EZ, A_ONEPE, A_LNZ, A_HI, A_MID0, A_LO0, A_MID1, A_LO1 = range(1, 11)
        PER_ACT = 10
        D_SP0, D_LOST, D_DELTA, D_DX = range(1, 5)
        PER_DVE = 4

        def wait(eng, s, v):
            if isinstance(v, int) and v <= 0:
                return
            eng.wait_ge(s, v)

        def flat(t3, l, c):
            return t3[:, c, :] if l == 0 else t3[:, :, :].rearrange("p (c two) n -> p c (two n)", two=2)[:, c, :]

        def schedule(eng, step):
            for l in range(LAYERS):
                last = CH[l] - 1
                step((l, 0, 0), None if l == 0 else (l - 1, CH[l - 1] - 1, 1), (l, 1, 1))
                if last - 1 > 2:
                    with eng.Fori(0, (last - 1) // 2) as pair:
                        c = pair * 2 + 1
                        step((l, c, 1), (l, c - 1, 0), (l, c + 1, 0))
                        step((l, c + 1, 0), (l, c, 1), (l, c + 2, 1))
                elif last > 1:
                    step((l, 1, 1), (l, 0, 0), (l, 2, 0))
                    step((l, 2, 0), (l, 1, 1), (l, 3, 1))
                step((l, last, 1), (l, last - 1, 0), (l + 1, 0, 0) if l + 1 < LAYERS else None)

        TILES = [(hg, t, s, 2 * hg + hp) for hg in range(2) for t in range(T) for s in range(2) for hp in range(2)]
        BY_POOL = [i % 8 in (2, 5, 7) for i in range(len(TILES))]
        BY_DVE = [i % 16 in (1, 6, 11) for i in range(len(TILES))]
        made = [sum(1 for o in BY_POOL[:i + 1] if o == BY_POOL[i]) for i in range(len(TILES))]
        sized = [sum(1 for o in BY_DVE[:i + 1] if o == BY_DVE[i]) for i in range(len(TILES))]

        def wait_diff(eng, i):
            eng.wait_ge(diff_pool if BY_POOL[i] else diff_dve, made[i])

        def wait_dist(eng, i):
            if i >= 0:
                eng.wait_ge(dist_dve if BY_DVE[i] else dist_act, sized[i])

        def batches(t3, s):
            return t3[:, :, :] if s is None else t3[:, 16 * s:16 * s + 16, 0:T]

        LATER = [(mean_w, "mean_w"), (w_q, "w_q"), (b_q, "b_q"), (w_k, "w_k"), (sel_k, "sel_k"), 
                 (b_v, "b_v"), (sel_key, "sel_key"), (key_rows, "key_rows"), (w_fan, "w_fan"), (b_fan, "b_fan"), (w_r1, "w_r1"),
                 (b_r1, "b_r1"), (w_r2, "w_r2"), (b_r2, "b_r2"), (lower, "lower"), (w_e1, "w_e1"), (b_e1, "b_e1"), (w_e2, "w_e2"),
                 (b_e2, "b_e2"), (w_e3, "w_e3"), (b_e3, "b_e3")]
        block = ctx.enter_context(nc.Block())

        def difference(engine, eng, i, tile):
            hg, t, s, hp = tile
            wait_dist(eng, i - RD)
            q = q_all[:, hp, s * HALF:(s + 1) * HALF].rearrange("p (b t) -> p b t", t=T)
            k = k_all[:, hp, s * HALF:(s + 1) * HALF].rearrange("p (b t) -> p b t", t=T)[:, :, t:t + 1].broadcast_to([128, HB, T])
            return engine.tensor_tensor(out=diff[:, i % RD, :].rearrange("p (b t) -> p b t", t=T), in0=q, in1=k, op=ALU.subtract)

        @block.sync
        def _(sp):
            sp.dma_start(x_l[0][:, 0, :], d["x"][:, 0:W]).then_inc(x_first, 16)
            sp.dma_start(w_ssm[:], d["w_ssm"]).then_inc(w_loaded, 16)
            sp.dma_start(vecs[:], d["vecs"]).then_inc(w_loaded, 16)
            sp.dma_start(sel_bc[:], d["sel_bc"]).then_inc(w_loaded, 16)
            sp.dma_start(a_neg[:], d["a_log"]).then_inc(w_loaded, 16)
            sp.dma_start(sel_red[:], d["sel_red"]).then_inc(w_loaded, 16)
            sp.dma_start(skip_w[:], d["skip_w"]).then_inc(w_loaded, 16)
            sp.dma_start(neg_id[:], d["neg_id"]).then_inc(w_loaded, 16)
            sp.dma_start(ident[:], d["ident"]).then_inc(w_loaded, 16)
            sp.dma_start(x_l[0][:, 1:CH[0], :], d["x"][:, W:].rearrange("p (c n) -> p c n", n=W)).then_inc(x_rest, 16)

            for tile, name in LATER:
                sp.dma_start(tile[:], d[name]).then_inc(weights_loaded, 16)

            def load_parts(l, c, slot):
                k = BASE[l] + c
                wait(sp, dx_bcast, PAIRS * (k - 1))
                for i, (piece, n) in enumerate(((hi, A_HI), (mid, A_MID1), (lo, A_LO1))):
                    sp.wait_ge(act_pre, PER_ACT * k + n)
                    for j in range(4):
                        sp.dma_start(parts[32 * i:32 * i + 32, slot, j, :, 0:W], piece[32 * j:32 * j + 32, :, 0:W])\
                          .then_inc(parts_loaded, 16)

            load_parts(0, 0, 0)

            def step(chunk, prev, nxt):
                if nxt:
                    load_parts(*nxt)
            schedule(sp, step)
            sp.wait_ge(y_copy, NCH)
            sp.dma_start(w_v[:], d["w_v"]).then_inc(w_v_loaded, 16)
            sp.wait_ge(final, 1)
            sp.dma_start(out, fin[:]).then_inc(stored, 16)
            sp.wait_ge(stored, 16)

        @block.scalar
        def _(act):
            act.preload_act_table_set("natural_log_exp_and_others")
            act.wait_ge(const_done, 1)
            nc.scalar.activation(a_neg[:], a_neg[:], ACT.Exp).then_inc(a_exp, 1)

            def prelude(l, c, slot, part):
                k = BASE[l] + c
                def done(n):
                    act.wait_ge(act_pre, PER_ACT * k + n)

                if part == 0:
                    wait(act, dve_pre, PER_DVE * k)
                    act.wait_ge(proj_done, 3 * k + 1)
                    nc.scalar.activation(z[:, 0:W], ps_proj[:, 0:W], ACT.Identity, bias=vecs[:, l, 1:2], scale=vecs[:, l, 0:1]).then_inc(act_pre, 1)
                    done(A_Z)
                    nc.scalar.activation(az[:, 0:W], z[:, 0:W], ACT.Abs).then_inc(act_pre, 1)
                elif part == 1:
                    wait(act, u_done, PAIRS * (k - 1))
                    act.wait_ge(proj_done, 3 * k + 2)
                    nc.scalar.activation(bmat[:, slot, :], ps_proj[:, 0:W], ACT.Copy).then_inc(proj_evac, 1)
                    done(A_AZ)
                    nc.scalar.activation(ez[:, 0:W], az[:, 0:W], ACT.Exp, scale=-1.0).then_inc(act_pre, 1)
                elif part == 2:
                    done(A_EZ)
                    nc.scalar.activation(onepe[:, 0:W], ez[:, 0:W], ACT.Identity, bias=1.0).then_inc(act_pre, 1)
                    nc.scalar.activation(lnz[:, 0:W], ez[:, 0:W], ACT.Ln, bias=1.0).then_inc(act_pre, 1)
                elif part == 3:
                    wait(act, prod_done, PAIRS * (k - 1))
                    act.wait_ge(proj_done, 3 * k + 3)
                    nc.scalar.activation(cmat[:, slot, :], ps_proj[:, 0:W], ACT.Copy).then_inc(proj_evac, 1)
                elif part == 4:
                    wait(act, parts_loaded, NDMA * k)
                    act.wait_ge(dve_pre, PER_DVE * k + D_DX)
                    nc.scalar.activation(hi[:, :, 0:W], src[:, :, 0:W], ACT.Copy).then_inc(act_pre, 1)
                else:
                    which, third = (part - 5) // 2, (part - 5) % 2
                    act.wait_ge(split_done, 4 * k + part - 4)
                    nc.scalar.activation((lo if third else mid)[:, which, 0:W], ps_proj[:, 0:W], ACT.Copy).then_inc(act_pre, 1)

            def finish(l, c, slot):
                k = BASE[l] + c
                act.wait_ge(reduce_done, PAIRS * (k + 1))
                if l < 2:
                    if not (isinstance(k, int) and k == 0):
                        act.wait_ge(pooled, k)
                    nc.scalar.activation(y_sb[:, 0:W], ps_y[:, 0:W], ACT.Copy, scale=0.5).then_inc(y_copy, 1)
                else:
                    nc.scalar.activation(h_tok[:, c * W:(c + 1) * W], ps_y[:, 0:W], ACT.Copy).then_inc(y_copy, 1)

            AT = {PRE + 1: 0, PRE + 4: 1, PRE + 5: 2, PRE + 7: 3, PRE + 9: 4, PRE + 12: 5, PRE + 14: 6, PRE + 17: 7, PRE + 19: 8}
            for part in range(9):
                prelude(0, 0, 0, part)

            def step(chunk, prev, nxt):
                l, c, slot = chunk
                k = BASE[l] + c
                if isinstance(c, int) and c == 0:
                    act.wait_ge(decay_zero, l + 1)
                for q in range(PAIRS):
                    G = PAIRS * k + q
                    wait(act, scan_done, G - RA + 1)
                    for r in range(2):
                        j = (2 * q + r) % 4
                        act.wait_ge(delta_bcast, 2 * G + r + 1)
                        e = 16 * j + q // 2
                        dst = decay[:, q % RA, r * W:(r + 1) * W].rearrange("p (b t) -> p b t", t=LEN[l])
                        s = ps_delta[:, r, 0:W].rearrange("p (b t) -> p b t", t=LEN[l])
                        nc.scalar.activation(dst[:, :, 1:], s[:, :, 1:], ACT.Exp, scale=a_neg[:, l, e:e + 1]).then_inc(exp_done, 1)
                    if prev and q == LAG:
                        finish(*prev)
                    if nxt and q in AT:
                        prelude(*nxt, AT[q])
            act.wait_ge(const_done, 2)
            schedule(act, step)
            finish(LAYERS - 1, CH[-1] - 1, 1)
            act.wait_ge(weights_loaded, 16 * len(LATER))

            def norm(n):
                for c in range(2):
                    cols = slice(c * COLS, (c + 1) * COLS)
                    act.wait_ge(ln["cent"], 2 * n + c + 1)
                    nc.scalar.activation(sq[:, cols], cent[:, cols], ACT.Square).then_inc(ln["sq"], 1)
                for c in range(2):
                    cols = slice(c * COLS, (c + 1) * COLS)
                    act.wait_ge(ln["eps"], 2 * n + c + 1)
                    nc.scalar.activation(rstd[:, cols], rstd[:, cols], ACT.Sqrt).then_inc(ln["sd"], 1)

            norm(0)
            for i in range(16):
                hp, s, c = i // 4, i // 2 % 2, i % 2
                act.wait_ge(q_proj, i + 1)
                nc.scalar.activation(q_all[:, hp, s * HALF + c * COLS:s * HALF + (c + 1) * COLS], P[:, 4 + i % 4, 0:COLS], ACT.Identity,
                                     bias=b_q[:, hp:hp + 1]).then_inc(q_ready, 1)

            def exps(hg):
                act.wait_ge(dist_used, len(TILES) // 2 * (hg + 1))
                act.wait_ge(pad_zero, 2)
                for i in range(4):
                    s, c = i // 2, i % 2
                    nc.scalar.activation(scores[:, hg, 32 * s + 16 * c:32 * s + 16 * c + 16, 0:T],
                                         P[:, 4 * hg + i, 0:COLS].rearrange("p (b t) -> p b t", t=T), ACT.Exp, scale=-0.125).then_inc(scores_exp, 1)

            for i in range(len(TILES)):
                if not BY_DVE[i]:
                    wait_diff(act, i)
                    wait(act, dist_used, i - RD + 1)
                    nc.scalar.activation(dist[:, i % RD, :], diff[:, i % RD, :], ACT.Abs).then_inc(dist_act, 1)
                if i == len(TILES) // 2 + 8:
                    exps(0)
            exps(1)
            for c in range(2):
                act.wait_ge(o_done, c + 1)
                nc.scalar.activation(sig[:, c, :], P[:, 4 + c, :], ACT.Sigmoid, scale=1.702).then_inc(sig_done, 1)
            norm(1)
            for c in range(2):
                act.wait_ge(r1_done, c + 1)
                nc.scalar.activation(rh[:, c * COLS:(c + 1) * COLS], P[0:64, 4 + c, 0:COLS], ACT.Relu, bias=b_r1[:, 0:1]).then_inc(rh_ready, 1)
            act.wait_ge(route, 3)
            nc.scalar.activation(prob[:], logit[:], ACT.Exp).then_inc(route_exp, 1)
            act.wait_ge(route, 6)
            nc.scalar.activation(gate[:], prob[:], ACT.Exp).then_inc(route_exp, 1)
            for i in range(24):
                layer, pair, s, c = i // 12, i // 4 % 3, i // 2 % 2, i % 2
                act.wait_ge(e12_done, i + 1)
                nc.scalar.activation((h2 if layer else h1)[:, pair, s, c * COLS:(c + 1) * COLS], P[:, i % 4, 0:COLS], ACT.Relu,
                                     bias=(b_e2 if layer else b_e1)[:, pair:pair + 1]).then_inc(e12_relu, 1)

        @block.vector
        def _(dve):
            dve.wait_ge(w_loaded, 128)
            nc.vector.tensor_scalar(out=a_neg[:], in0=a_neg[:], scalar1=80.0, scalar2=None, op0=ALU.min).then_inc(const_done, 1)
            dve.wait_ge(a_exp, 1)
            nc.vector.tensor_scalar(out=a_neg[:], in0=a_neg[:], scalar1=-1.0, scalar2=None, op0=ALU.mult).then_inc(const_done, 1)
            def prelude(l, c, slot, part):
                k = BASE[l] + c
                if part == 0:
                    dve.wait_ge(act_pre, PER_ACT * k + A_LNZ)
                    nc.vector.scalar_tensor_tensor(out=sp0[:, 0:W], in0=z[:, 0:W], scalar=0.0, in1=lnz[:, 0:W], op0=ALU.max, op1=ALU.add).then_inc(dve_pre, 1)
                    nc.vector.scalar_tensor_tensor(out=lost[:, 0:W], in0=onepe[:, 0:W], scalar=1.0, in1=ez[:, 0:W], op0=ALU.subtract, op1=ALU.subtract).then_inc(dve_pre, 1)
                elif part == 1:
                    dve.wait_ge(dve_pre, PER_DVE * k + D_LOST)
                    nc.vector.tensor_tensor(out=src[:, 0, 0:W], in0=sp0[:, 0:W], in1=lost[:, 0:W], op=ALU.subtract).then_inc(dve_pre, 1)
                else:
                    dve.wait_ge(dve_pre, PER_DVE * k + D_DELTA)
                    nc.vector.tensor_tensor(out=src[:, 1, 0:W], in0=src[:, 0, 0:W], in1=flat(x_l[l], l, c), op=ALU.mult).then_inc(dve_pre, 1)

            AT = {PRE + 6: 0, PRE + 7: 1, PRE + 8: 2}
            dve.wait_ge(x_first, 16)
            for part in range(3):
                prelude(0, 0, 0, part)
            dve.wait_ge(x_rest, 16)

            def finish(l, c, slot):
                if l < 2:
                    k = BASE[l] + c
                    dve.wait_ge(y_copy, k + 1)
                    pairs = y_sb[:, 0:W].rearrange("p (b t) -> p b t", t=LEN[l])[:, :, 0:2 * LEN[l + 1]].rearrange("p b (t two) -> p b t two", two=2)
                    dst = x_l[l + 1][:, c, :].rearrange("p (b t) -> p b t", t=LEN[l + 1])
                    nc.vector.tensor_tensor(out=dst, in0=pairs[:, :, :, 0], in1=pairs[:, :, :, 1], op=ALU.add).then_inc(pooled, 1)

            def inputs(l, k, slot, q):
                G = PAIRS * k + q
                dve.wait_ge(dx_bcast, G + 1)
                wait(dve, prod_done, G - RH + 1)
                dst = h[:, q % RH, :].rearrange("p (r n) -> p r n", r=2)
                nc.vector.tensor_tensor(out=dst, in0=ps_dx[:, q % 2, :, 0:W], in1=bmat[:, slot, :].unsqueeze(1).broadcast_to([128, 2, W]), op=ALU.mult)\
                  .then_inc(u_done, 1)

            def step(chunk, prev, nxt):
                l, c, slot = chunk
                k = BASE[l] + c
                if isinstance(c, int) and c == 0:
                    wait(dve, scan_done, PAIRS * k)
                    for a in range(RA):
                        dst = decay[:, a, :].rearrange("p (b t) -> p b t", t=LEN[l])[:, :, 0:1]
                        last = nc.vector.memset(dst, 0.0)
                    last.then_inc(decay_zero, 1)
                dve.wait_ge(proj_evac, 2 * k + 1)
                inputs(l, k, slot, 0)
                for q in range(PAIRS):
                    G = PAIRS * k + q
                    if q + 1 < PAIRS:
                        inputs(l, k, slot, q + 1)
                    dve.wait_ge(u_done, G + 1)
                    dve.wait_ge(exp_done, 2 * G + 2)
                    nc.vector.tensor_tensor_scan(out=h[:, q % RH, :], data0=decay[:, q % RA, :], data1=h[:, q % RH, :],
                                                 initial=0.0, op0=ALU.mult, op1=ALU.add).then_inc(scan_done, 1)
                    if prev and q == LAG:
                        finish(*prev)
                    if nxt and q in AT:
                        prelude(*nxt, AT[q])
            dve.wait_ge(const_done, 2)
            schedule(dve, step)
            dve.wait_ge(weights_loaded, 16 * len(LATER))

            def norm(n, x, dst, after):
                for c in range(2):
                    cols = slice(c * COLS, (c + 1) * COLS)
                    dve.wait_ge(ln["mean"], 2 * n + c + 1)
                    nc.vector.tensor_tensor(out=cent[:, cols], in0=x[:, cols], in1=P[:, c, 0:COLS], op=ALU.subtract).then_inc(ln["cent"], 1)
                for c in range(2):
                    cols = slice(c * COLS, (c + 1) * COLS)
                    dve.wait_ge(ln["var"], 2 * n + c + 1)
                    nc.vector.tensor_scalar(out=rstd[:, cols], in0=P[:, 2 + c, 0:COLS], scalar1=EPS, scalar2=None, op0=ALU.add).then_inc(ln["eps"], 1)
                for c in range(2):
                    cols = slice(c * COLS, (c + 1) * COLS)
                    dve.wait_ge(ln["sd"], 2 * n + c + 1)
                    nc.vector.reciprocal(sq[:, cols], rstd[:, cols]).then_inc(ln["rstd"], 1)
                    dve.wait_ge(ln["rstd"], 2 * n + c + 1)
                    nc.vector.tensor_tensor(out=dst(c), in0=cent[:, cols].rearrange("p (b t) -> p b t", t=T),
                                            in1=sq[:, cols].rearrange("p (b t) -> p b t", t=T), op=ALU.mult).then_inc(ln["out"], 1)

            dve.wait_ge(y_copy, NCH)
            dve.wait_ge(reduce_done, PAIRS * NCH)
            nc.vector.memset(normed[:, :, T:32], 0.0).then_inc(pad_zero, 1)
            nc.vector.memset(scores[:, :, :, T:32], 0.0).then_inc(pad_zero, 1)
            norm(0, h_tok, lambda c: normed[:, 16 * c:16 * c + 16, 0:T], 0)
            dve.wait_ge(ln["out"], 2)
            nc.vector.tensor_tensor(out=res[:, :].rearrange("p (b t) -> p b t", t=T), in0=h_tok[:, :].rearrange("p (b t) -> p b t", t=T),
                                    in1=normed[:, :, 0:T], op=ALU.add).then_inc(h_ready, 1)
            for hp in range(NHP):
                for i in range(4):
                    dve.wait_ge(k_proj, i + 1)
                    nc.vector.tensor_scalar(out=k_all[:, hp, i * COLS:(i + 1) * COLS], in0=P[:, i, 0:COLS], scalar1=w_k[:, hp:hp + 1], scalar2=None,
                                            op0=ALU.mult).then_inc(k_ready, 1)
            dve.wait_ge(k_ready, 16)
            dve.wait_ge(q_ready, 16)

            def soft(hg):
                dve.wait_ge(scores_exp, 4 * (hg + 1))
                sc = scores[:, hg, :, :]
                nc.vector.reduce_sum(esum[:, hg, :], sc, AX.X).then_inc(softmax, 1)
                dve.wait_ge(softmax, 6 * hg + 1)
                nc.vector.tensor_scalar(out=esum[:, hg, :], in0=esum[:, hg, :], scalar1=1.0, scalar2=None, op0=ALU.add).then_inc(softmax, 1)
                dve.wait_ge(softmax, 6 * hg + 2)
                nc.vector.reciprocal(esum[:, hg, :], esum[:, hg, :]).then_inc(softmax, 1)
                dve.wait_ge(softmax, 6 * hg + 3)
                nc.vector.tensor_scalar(out=esum[:, hg, :], in0=esum[:, hg, :], scalar1=key_rows[:, 0:1], scalar2=None, op0=ALU.mult).then_inc(softmax, 1)
                dve.wait_ge(softmax, 6 * hg + 4)
                nc.vector.tensor_tensor(out=sc, in0=sc, in1=esum[:, hg, :].unsqueeze(2).broadcast_to([128, BATCH, 32]), op=ALU.mult).then_inc(softmax, 1)
                dve.wait_ge(softmax, 6 * hg + 5)
                nc.vector.transpose(scores_t[:, hg, :, :].rearrange("p b t -> p (b t)"), sc.rearrange("p b t -> p (b t)")).then_inc(softmax, 1)

            def size(i):
                if i >= 0 and BY_DVE[i]:
                    wait_diff(dve, i)
                    wait(dve, dist_used, i - RD + 1)
                    nc.vector.tensor_scalar(out=dist[:, i % RD, :].bitcast(U32), in0=diff[:, i % RD, :].bitcast(U32), scalar1=0x7FFFFFFF, scalar2=None,
                                            op0=ALU.bitwise_and).then_inc(dist_dve, 1)

            for i, tile in enumerate(TILES):
                if not BY_POOL[i]:
                    difference(nc.vector, dve, i, tile).then_inc(diff_dve, 1)
                size(i - 1)
                if i == len(TILES) // 2 + 24:
                    soft(0)
            size(len(TILES) - 1)
            soft(1)
            for i in range(32):
                dve.wait_ge(v_proj, i + 1)
                nc.vector.tensor_tensor(out=v_all[:, 2 * i:2 * i + 2, :, :, :].rearrange("p b f g w -> p b (f g w)"), in0=P[:, i % 4, :].rearrange("p (b n) -> p b n", b=2),
                                        in1=b_v[:, :].unsqueeze(1).broadcast_to([128, 2, 256]), op=ALU.add).then_inc(v_ready, 1)
            for c in range(2):
                dve.wait_ge(sig_done, c + 1)
                nc.vector.tensor_tensor(out=gated[:, 16 * c:16 * c + 16, :].rearrange("p b t -> p (b t)"), in0=P[:, 4 + c, :], in1=sig[:, c, :], op=ALU.mult).then_inc(gated_done, 1)
            dve.wait_ge(h_ready, 1)
            for c in range(2):
                cols = slice(c * COLS, (c + 1) * COLS)
                dve.wait_ge(fan_done, c + 1)
                nc.vector.scalar_tensor_tensor(out=h_att[:, cols], in0=P[:, 6 + c, 0:COLS], scalar=b_fan[:, 0:1], in1=res[:, cols], op0=ALU.add, op1=ALU.add).then_inc(att_done, 1)
            dve.wait_ge(att_done, 2)
            norm(1, h_att, lambda c: f_in[:, c * COLS:(c + 1) * COLS].rearrange("p (b t) -> p b t", t=T), 0)

            link = [0]

            def chained(ins):
                link[0] += 1
                ins.then_inc(route, 1)
                dve.wait_ge(route, link[0])

            def per_expert(v):
                return v.unsqueeze(2).broadcast_to([TT, 16, NE])

            dve.wait_ge(r2_done, 1)
            chained(nc.vector.tensor_tensor(out=logit[:], in0=P[0:TT, 7, 0:96].rearrange("p (k e) -> p k e", e=NE),
                                            in1=b_r2[:, :].unsqueeze(1).broadcast_to([TT, 16, NE]), op=ALU.add))
            chained(nc.vector.reduce_max(stat[:, 0, :], logit[:], AX.X))
            chained(nc.vector.tensor_tensor(out=logit[:], in0=logit[:], in1=per_expert(stat[:, 0, :]), op=ALU.subtract))
            dve.wait_ge(route_exp, 1)
            chained(nc.vector.reduce_sum(stat[:, 1, :], prob[:], AX.X))
            chained(nc.vector.reciprocal(stat[:, 2, :], stat[:, 1, :]))
            chained(nc.vector.tensor_tensor(out=prob[:], in0=prob[:], in1=per_expert(stat[:, 2, :]), op=ALU.mult))
            for n, op in ((0, ALU.is_ge), (1, ALU.is_gt)):
                for e in range(NE):
                    chained(nc.vector.tensor_tensor(out=beats[:, n, :, e * NE:(e + 1) * NE], in0=prob[:], in1=prob[:, :, e:e + 1].broadcast_to([TT, 16, NE]), op=op))
                chained(nc.vector.tensor_tensor(out=beats[:, n, :, :], in0=beats[:, n, :, :], in1=lower[:, n, :, :].rearrange("p a b -> p (a b)").unsqueeze(1).broadcast_to([TT, 16, NE * NE]), op=ALU.mult))
            chained(nc.vector.tensor_tensor(out=beats[:, 0, :, :], in0=beats[:, 0, :, :], in1=beats[:, 1, :, :], op=ALU.add))
            chained(nc.vector.reduce_sum(rank[:].rearrange("p k e -> p (k e)"), beats[:, 0, :, :].rearrange("p k (i j) -> p (k i) j", j=NE), AX.X))
            chained(nc.vector.tensor_scalar(out=rank[:], in0=rank[:], scalar1=2.0, scalar2=None, op0=ALU.is_lt))
            dve.wait_ge(route_exp, 2)
            chained(nc.vector.tensor_tensor(out=gate[:], in0=gate[:], in1=rank[:], op=ALU.mult))
            chained(nc.vector.reduce_sum(stat[:, 3, :], gate[:], AX.X))
            chained(nc.vector.reciprocal(stat[:, 0, :], stat[:, 3, :]))
            chained(nc.vector.tensor_tensor(out=gate[:], in0=gate[:], in1=per_expert(stat[:, 0, :]), op=ALU.mult))

            def experts(v):
                return v.rearrange("p (e o) -> p e o", e=NE)

            def weigh(i):
                dve.wait_ge(e3_used, i + 1)
                nc.vector.tensor_tensor(out=experts(eo[:, i % 3, :]), in0=experts(eo[:, i % 3, :]), in1=gate[:, i, :].unsqueeze(2).broadcast_to([TT, NE, D]),
                                        op=ALU.mult).then_inc(mixing, 1)

            def collect(i):
                dve.wait_ge(mixing, i + 1)
                nc.vector.reduce_sum(mix[:, i, :], eo[:, i % 3, :].rearrange("p (e o) -> p o e", e=NE), AX.X).then_inc(mixed, 1)

            for i in range(16):
                dve.wait_ge(e3_done, i + 1)
                wait(dve, mixed, i - 2)
                nc.vector.tensor_tensor(out=eo[:, i % 3, :], in0=P[0:TT, 4 + i % 3, 0:NE * D], in1=b_e3[:], op=ALU.add).then_inc(e3_used, 1)
                if i:
                    weigh(i - 1)
                if i > 1:
                    collect(i - 2)
            weigh(15)
            collect(14)
            collect(15)
            dve.wait_ge(back, 8)
            dve.wait_ge(mixed, 16)
            for c in range(2):
                for s in range(2):
                    def tiles(t3):
                        return t3[:, 8 * c:8 * c + 8, :].rearrange("p (k s) (j l) -> p s k j l", s=2, j=4)[:, s, :, :, :]
                    last = nc.vector.tensor_tensor(out=tiles(fin), in0=tiles(mix), in1=P[0:TT, c, :].rearrange("p (k j s l) -> p s k j l", k=4, j=4, s=2)[:, s, :, :, :], op=ALU.add)
            last.then_inc(final, 1)

        @block.gpsimd
        def _(pool):
            def step(chunk, prev, nxt):
                l, c, slot = chunk
                k = BASE[l] + c
                pool.wait_ge(proj_evac, 2 * k + 2)
                for q in range(PAIRS):
                    G = PAIRS * k + q
                    pool.wait_ge(scan_done, G + 1)
                    wait(pool, reduce_done, G - RG + 1)
                    nc.gpsimd.tensor_tensor(out=g[:, q % RG, :].rearrange("p (r n) -> p r n", r=2), in0=h[:, q % RH, :].rearrange("p (r n) -> p r n", r=2),
                                            in1=cmat[:, slot, :].unsqueeze(1).broadcast_to([128, 2, W]), op=ALU.mult).then_inc(prod_done, 1)
            schedule(pool, step)
            pool.wait_ge(k_ready, 16)
            pool.wait_ge(q_ready, 16)
            for i, tile in enumerate(TILES):
                if BY_POOL[i]:
                    difference(nc.gpsimd, pool, i, tile).then_inc(diff_pool, 1)

        @block.tensor
        def _(pe):
            pe.wait_ge(w_loaded, 128)
            pe.wait_ge(x_first, 16)

            HALVES = (slice(0, W // 2), slice(W // 2, W))

            def project(l, c, slot, part, half):
                k = BASE[l] + c
                cols = HALVES[half]
                if part < 3:
                    if part == 0:
                        if l > 0:
                            pe.wait_ge(pooled, BASE[l - 1] + 2 * c + 2)
                        wait(pe, act_pre, PER_ACT * k)
                    elif part == 1:
                        pe.wait_ge(act_pre, PER_ACT * k + A_Z)
                    else:
                        pe.wait_ge(proj_evac, 2 * k + 1)
                    last = nc.tensor.matmul(ps_proj[:, cols], w_ssm[:, l, (2, 0, 1)[part], :], flat(x_l[l], l, c)[:, cols], start=True, stop=True)
                    if half:
                        last.then_inc(proj_done, 1)
                elif part in (3, 5):
                    which = (part - 3) // 2
                    pe.wait_ge(act_pre, PER_ACT * k + (A_LO0 if which else A_HI))
                    pe.wait_ge(proj_evac, 2 * k + 2)
                    nc.tensor.matmul(ps_proj[:, cols], ident[:], src[:, which, cols], start=(half == 0), stop=False, skip_group_check=True)
                    last = nc.tensor.matmul(ps_proj[:, cols], neg_id[:], hi[:, which, cols], start=False, stop=True, skip_group_check=True)
                    if half:
                        last.then_inc(split_done, 1)
                elif half:
                    which = (part - 4) // 2
                    pe.wait_ge(act_pre, PER_ACT * k + (A_MID1 if which else A_MID0))
                    for cols in HALVES:
                        last = nc.tensor.matmul(ps_proj[:, cols], neg_id[:], mid[:, which, cols], start=False, stop=True, skip_group_check=True)
                    last.then_inc(split_done, 1)

            for part in range(7):
                for half in range(2):
                    project(0, 0, 0, part, half)
            pe.wait_ge(x_rest, 16)

            def reduce(l, c, slot, q):
                pe.wait_ge(prod_done, PAIRS * (BASE[l] + c) + q + 1)
                if q < 2:
                    if q == 0:
                        wait(pe, y_copy, BASE[l] + c)
                    cols = HALVES[q]
                    nc.tensor.matmul(ps_y[:, cols], skip_w[:, l, :], flat(x_l[l], l, c)[:, cols], start=(q == 0), stop=False, skip_group_check=True)
                for r in range(2):
                    j = (2 * q + r) % 4
                    last = nc.tensor.matmul(ps_y[32 * j:32 * j + 32, 0:W], sel_red[:, q // 2, :], g[:, q % RG, r * W:(r + 1) * W],
                                            start=False, stop=(q // 2 == 15), tile_position=(0, 32 * j), skip_group_check=True)
                last.then_inc(reduce_done, 1)

            AT = {PRE: (0, 0), PRE + 1: (0, 1), PRE + 3: (1, 0), PRE + 4: (1, 1), PRE + 6: (2, 0), PRE + 7: (2, 1), PRE + 10: (3, 0), PRE + 11: (3, 1),
                  PRE + 13: (4, 1), PRE + 15: (5, 0), PRE + 16: (5, 1), PRE + 18: (6, 1)}

            def step(chunk, prev, nxt):
                l, c, slot = chunk
                k = BASE[l] + c
                pe.wait_ge(parts_loaded, NDMA * (k + 1))
                for q in range(PAIRS):
                    G = PAIRS * k + q
                    el = q // 2
                    wait(pe, u_done, G - 1)
                    for r in range(2):
                        last = nc.tensor.matmul(ps_dx[:, q % 2, r, 0:W], sel_bc[:, el, :], parts[:, slot, (2 * q + r) % 4, 1, :], start=True, stop=True)
                    last.then_inc(dx_bcast, 1)
                    for r in range(2):
                        wait(pe, exp_done, 2 * G + r - 1)
                        nc.tensor.matmul(ps_delta[:, r, 0:W], sel_bc[:, el, :], parts[:, slot, (2 * q + r) % 4, 0, :], start=True, stop=True).then_inc(delta_bcast, 1)
                    if q >= LAG:
                        reduce(l, c, slot, q - LAG)
                    elif prev:
                        reduce(*prev, PAIRS - LAG + q)
                    if nxt and q in AT:
                        project(*nxt, *AT[q])
            schedule(pe, step)
            for q in range(PAIRS - LAG, PAIRS):
                reduce(LAYERS - 1, CH[-1] - 1, 1, q)
            pe.wait_ge(weights_loaded, 16 * len(LATER))

            def norm(n, x, ready, count):
                for c in range(2):
                    pe.wait_ge(ready, count)
                    nc.tensor.matmul(P[:, c, 0:COLS], mean_w[:], x[:, c * COLS:(c + 1) * COLS], start=True, stop=True).then_inc(ln["mean"], 1)
                for c in range(2):
                    pe.wait_ge(ln["sq"], 2 * n + c + 1)
                    nc.tensor.matmul(P[:, 2 + c, 0:COLS], mean_w[:], sq[:, c * COLS:(c + 1) * COLS], start=True, stop=True).then_inc(ln["var"], 1)

            norm(0, h_tok, y_copy, NCH)
            pe.wait_ge(ln["out"], 2)
            for i in range(4):
                s, c = i // 2, i % 2
                nc.tensor.matmul(P[:, i, 0:COLS], sel_k[:, s, :], normed[:, 16 * c:16 * c + 16, 0:T], start=True, stop=True).then_inc(k_proj, 1)
            for i in range(16):
                hp, s, c = i // 4, i // 2 % 2, i % 2
                wait(pe, q_ready, i - 3)
                nc.tensor.matmul(P[:, 4 + i % 4, 0:COLS], w_q[:, s, hp, :], normed[:, 16 * c:16 * c + 16, 0:T], start=True, stop=True).then_inc(q_proj, 1)
            pe.wait_ge(k_ready, 16)
            for i, (hg, t, s, hp) in enumerate(TILES):
                if i == len(TILES) // 2:
                    pe.wait_ge(q_ready, 16)
                wait_dist(pe, i)
                lo_row = 64 * (hp % 2)
                for c in range(2):
                    last = nc.tensor.matmul(P[lo_row:lo_row + 64, 4 * hg + 2 * s + c, 0:COLS], sel_key[:, t, :], dist[:, i % RD, c * COLS:(c + 1) * COLS],
                                            start=(t == 0), stop=(t == T - 1), tile_position=(0, lo_row))
                last.then_inc(dist_used, 1)
            pe.wait_ge(w_v_loaded, 16)
            pe.wait_ge(pad_zero, 1)
            pe.wait_ge(scores_exp, 4)
            for i in range(32):
                wait(pe, v_ready, i - 3)
                for b in (2 * i, 2 * i + 1):
                    for h4 in range(4):
                        last = nc.tensor.matmul(P[32 * h4:32 * h4 + 32, i % 4, 256 * (b % 2):256 * (b % 2) + 256], normed[:, b % HB, :], w_v[:, b // HB, h4, :],
                                                start=True, stop=True, tile_position=(0, 32 * h4))
                last.then_inc(v_proj, 1)
            pe.wait_ge(softmax, 12)
            pe.wait_ge(scores_exp, 8)
            pe.wait_ge(v_ready, 32)
            for b32 in range(HB):
                for s in range(2):
                    b = s * HB + b32
                    for n, (f, hg) in enumerate(((0, 0), (0, 1), (1, 0), (1, 1))):
                        last = nc.tensor.matmul(P[64 * s:64 * s + 64, 4 + b32 // 16, 32 * (b32 % 16):32 * (b32 % 16) + 32], v_all[:, b, f, hg, :],
                                                (scores if f else scores_t)[:, hg, b, :], start=(n == 0), stop=(n == 3), tile_position=(0, 64 * s))
                if b32 % 16 == 15:
                    last.then_inc(o_done, 1)
            for c in range(2):
                pe.wait_ge(gated_done, c + 1)
                nc.tensor.matmul(P[:, 6 + c, 0:COLS], w_fan[:], gated[:, 16 * c:16 * c + 16, 0:T], start=True, stop=True).then_inc(fan_done, 1)
            norm(1, h_att, att_done, 2)
            pe.wait_ge(ln["out"], 4)
            for c in range(2):
                nc.tensor.matmul(P[0:64, 4 + c, 0:COLS], w_r1[:], f_in[:, c * COLS:(c + 1) * COLS], start=True, stop=True).then_inc(r1_done, 1)
            pe.wait_ge(rh_ready, 2)
            for k in range(8):
                last = nc.tensor.matmul(P[0:TT, 7, 2 * NE * k:2 * NE * (k + 1)], rh[:, TT * k:TT * (k + 1)], w_r2[:], start=True, stop=True)
            last.then_inc(r2_done, 1)
            for i in range(24):
                layer, pair, s, c = i // 12, i // 4 % 3, i // 2 % 2, i % 2
                cols = slice(c * COLS, (c + 1) * COLS)
                wait(pe, e12_relu, max(i - 3, i - 11 if layer else 0))
                nc.tensor.matmul(P[:, i % 4, 0:COLS], w_e2[:, pair, :] if layer else w_e1[:, s, pair, :], h1[:, pair, s, cols] if layer else f_in[:, cols],
                                 start=True, stop=True).then_inc(e12_done, 1)
            pe.wait_ge(e12_relu, 24)
            for i in range(16):
                k, s = i // 2, i % 2
                wait(pe, e3_used, i - 2)
                for pair in range(NE // 2):
                    last = nc.tensor.matmul(P[0:TT, 4 + i % 3, 128 * pair:128 * pair + 128], h2[:, pair, s, TT * k:TT * (k + 1)], w_e3[:, pair, :], start=True, stop=True)
                last.then_inc(e3_done, 1)
            for k in range(8):
                nc.tensor.transpose(P[0:TT, k // 4, 128 * (k % 4):128 * (k % 4) + 128], h_att[:, TT * k:TT * (k + 1)], ident[:]).then_inc(back, 1)


def lay_out(i):
    f = np.float32
    e = np.arange(D)
    def chan(a):
        a = np.asarray(a)
        return np.repeat(a.reshape(4, 1, 16, *a.shape[1:]), 2, axis=1).reshape(128, *a.shape[1:])
    half_of = np.repeat(np.tile(np.arange(2), 4), 16)
    o = {}
    x = np.asarray(i["x"]).reshape(2, HB, SEQ, 4, 16)[:, :, :LEN[0]]
    o["x"] = np.ascontiguousarray(x.transpose(3, 0, 4, 1, 2).reshape(128, HB * LEN[0]))
    w = np.zeros((128, LAYERS, 3, 128), f)
    for l in range(LAYERS):
        wd = np.asarray(i["L0_tok_W_dbc"][l])
        for s in range(2):
            rows = half_of == s
            for part, block in ((0, wd[1:65]), (1, wd[65:129])):
                w[rows, l, part, 64 * s:64 * s + 64] = chan(block.T)[rows]
            w[np.ix_(rows, [l], [2], rows)] = chan(wd[0])[rows][:, None, None, None]
    o["w_ssm"] = w
    v = np.zeros((128, LAYERS, 2), f)
    o["skip_w"] = np.zeros((128, LAYERS, 128), f)
    for l in range(LAYERS):
        v[:, l, 0] = chan(i["L0_tok_W_dt"][l][:, 0])
        v[:, l, 1] = chan(i["L0_tok_b_dt"][l])
        o["skip_w"][np.arange(128), l, np.arange(128)] = chan(i["L0_tok_D"][l])
    o["vecs"] = v
    al = np.asarray(i["L0_tok_A_log"]).transpose(2, 0, 1)
    o["a_log"] = np.concatenate([al, al], axis=0)
    wq = np.asarray(i["L0_attn_wqv_w"]).reshape(3, 4, 2, D, D)
    o["w_q"] = np.zeros((128, 2, NHP, 128), f)
    o["w_v"] = np.zeros((128, 2, 4, 2, 2, D), f)
    wv = np.asarray(i["L0_attn_wqv_w"]).reshape(3, 2, 4, D, D)[1:]
    o["w_e1"] = np.zeros((128, 2, NE // 2, 128), f)
    o["w_r1"] = np.zeros((128, 2, 32), f)
    o["w_fan"] = np.zeros((2, D, 128), f)
    for s in range(2):
        rows = half_of == s
        o["w_q"][rows, s] = chan(wq[0].transpose(3, 0, 1, 2).reshape(D, NHP, 128))[rows]
        o["w_v"][rows, s] = chan(wv.transpose(4, 2, 0, 1, 3))[rows]
        o["w_e1"][rows, s] = chan(np.asarray(i["L0_ffn_expert_w1"]).transpose(1, 0, 2).reshape(D, NE // 2, 128))[rows]
        o["w_r1"][rows, s] = chan(i["L0_ffn_router_w1"])[rows]
        o["w_fan"][s][:, rows] = chan(i["L0_attn_fanin_w"])[rows].T
    o["w_v"] = o["w_v"].reshape(128, 2, 4, 256)
    o["w_r1"] = o["w_r1"].reshape(128, 64)
    o["w_fan"] = o["w_fan"].reshape(128, 128)
    bq = np.asarray(i["L0_attn_wqv_b"]).reshape(3, 4, 128)
    o["b_q"] = bq[0].T
    o["w_k"] = np.asarray(i["L0_attn_wk"]).reshape(4, 128).T
    bv = np.asarray(i["L0_attn_wqv_b"]).reshape(3, 2, 4, 1, D)[1:].transpose(2, 3, 0, 1, 4)
    o["b_v"] = np.broadcast_to(bv, (4, 32, 2, 2, D)).reshape(128, 256)
    o["b_fan"] = chan(i["L0_attn_fanin_b"])[:, None]
    o["b_r1"] = np.tile(np.asarray(i["L0_ffn_router_b1"]), 2)[:, None]
    o["w_r2"] = np.zeros((2, 32, 2, NE), f)
    for s in range(2):
        o["w_r2"][s, :, s] = i["L0_ffn_router_w2"]
    o["w_r2"] = o["w_r2"].reshape(64, 2 * NE)
    o["b_r2"] = np.broadcast_to(np.asarray(i["L0_ffn_router_b2"]), (TT, NE))
    for n in (2, 3):
        w = np.zeros((2, D, NE // 2, 2, D), f)
        for e in range(NE):
            w[e % 2, :, e // 2, e % 2] = i[f"L0_ffn_expert_w{n}"][e]
        o[f"w_e{n}"] = w.reshape(128, NE // 2, 128)
    for n in (1, 2):
        o[f"b_e{n}"] = np.asarray(i[f"L0_ffn_expert_b{n}"]).reshape(NE // 2, 128).T
    o["b_e3"] = np.broadcast_to(np.asarray(i["L0_ffn_expert_b3"]).reshape(1, NE * D), (TT, NE * D))
    return o


def constants():
    f = np.float32
    o = {}
    s = np.zeros((2, 64, 16, 2, 16), f)
    for h in range(2):
        for el in range(16):
            s[h, :, el, h, el] = 1.0
    o["sel_red"] = s.reshape(128, 16, 32)
    o["neg_id"] = -np.eye(128, dtype=f).astype(np.dtype("bfloat16"))
    b = np.zeros((3, 2, 16, 16, 2, 64), f)
    for h in range(2):
        for el in range(16):
            b[:, h, el, el, h, :] = 1.0
    o["sel_bc"] = b.reshape(96, 16, 128).astype(np.dtype("bfloat16"))
    half_of = np.repeat(np.tile(np.arange(2), 4), 16)
    chan_of = (np.arange(4)[:, None, None] * 16 + np.zeros((1, 2, 1), int) + np.arange(16)).reshape(128)
    o["mean_w"] = ((half_of[:, None] == half_of[None, :]) / D).astype(f)
    o["ident"] = np.eye(128, dtype=f)
    o["sel_k"] = np.stack([((half_of == s)[:, None] & (chan_of[:, None] == np.tile(np.arange(D), 2)[None, :])) for s in range(2)], axis=1).astype(f)
    k = np.zeros((2, D, T, 2, 32), f)
    for h in range(2):
        for t in range(T):
            k[h, :, t, h, t] = 1.0
    o["sel_key"] = k.reshape(128, T, 64)
    o["key_rows"] = (np.arange(128) % 32 < T).astype(f)[:, None]
    own, other = np.meshgrid(np.arange(NE), np.arange(NE), indexing="ij")
    o["lower"] = np.broadcast_to(np.stack([other < own, other > own]).astype(f), (TT, 2, NE, NE))
    return o


def kernel(**inputs):
    import concourse.bacc as _bacc
    from concourse import mybir as _mybir
    from concourse.bass_utils import run_bass_kernel_spmd as _run
    nc = _bacc.Bacc("TRN2", target_bir_lowering=False, num_devices=1)
    arrays = {k: np.ascontiguousarray(v) for k, v in {**lay_out(inputs), **constants()}.items()}
    d = {k: nc.dram_tensor("in_" + k, a.shape, _mybir.dt.from_np(a.dtype), kind="ExternalInput").ap() for k, a in arrays.items()}
    out = nc.dram_tensor("out", (TT, 16, D), _mybir.dt.float32, kind="ExternalOutput").ap()
    build(nc, d, out)
    r = _run(nc, [{"in_" + k: a for k, a in arrays.items()}], core_ids=[0])
    o = r.results[0]["out"].reshape(4, T, 8, 2, D)
    return np.ascontiguousarray(o.transpose(3, 2, 0, 1, 4).reshape(BATCH, T, D))
```

```python
import concourse.bass as bass
from concourse import mybir
from contextlib import ExitStack
import numpy as np

BATCH, SEQ, D, NS, LAYERS = 64, 125, 64, 64, 3
HB = BATCH // 2
LEN = [SEQ // 4 * 4, SEQ // 4 * 2, SEQ // 4]
CB = [4, 8, 16]
W = CB[0] * LEN[0]
assert all(CB[l] * LEN[l] == W for l in range(LAYERS)) and SEQ // 2 // 2 == SEQ // 4
CH = [HB // CB[l] for l in range(LAYERS)]
BASE = [0, CH[0], CH[0] + CH[1]]
NCH = sum(CH)
PAIRS = D // 2
T = LEN[2]
HALF = HB * T
COLS = HALF // 2
NHP = 4
NE = 6
TT = 4 * T
EPS = 1e-5


def build(nc, d, out):
    F = mybir.dt.float32
    BF = mybir.dt.bfloat16
    ALU = mybir.AluOpType
    U32 = mybir.dt.uint32
    ACT = mybir.ActivationFunctionType
    AX = mybir.AxisListType
    ctx = ExitStack()
    ssm = ExitStack()
    with ctx:
        def sb(name, shape, dt=F, stack=ctx):
            return stack.enter_context(nc.sbuf_tensor(name, shape, dt))

        def sem(name):
            return ctx.enter_context(nc.semaphore(name))

        h_tok = sb("h_tok", [128, HALF])
        mean_w = sb("mean_w", [128, 128])
        ident = sb("ident", [128, 128])
        w_q = sb("w_q", [128, 2, NHP, 128])
        b_q = sb("b_q", [128, NHP])
        w_k = sb("w_k", [128, NHP])
        sel_k = sb("sel_k", [128, 2, 128])
        b_v = sb("b_v", [128, 256])
        sel_key = sb("sel_key", [128, T, 64])
        key_rows = sb("key_rows", [128, 1])
        w_fan = sb("w_fan", [128, 128])
        b_fan = sb("b_fan", [128, 1])
        w_r1 = sb("w_r1", [128, 64])
        b_r1 = sb("b_r1", [64, 1])
        w_r2 = sb("w_r2", [64, 2 * NE])
        b_r2 = sb("b_r2", [TT, NE])
        lower = sb("lower", [TT, 2, NE, NE])
        w_e1 = sb("w_e1", [128, 2, NE // 2, 128])
        b_e1 = sb("b_e1", [128, NE // 2])
        w_e2 = sb("w_e2", [128, NE // 2, 128])
        b_e2 = sb("b_e2", [128, NE // 2])
        w_e3 = sb("w_e3", [128, NE // 2, 128])
        b_e3 = sb("b_e3", [TT, NE * D])

        def sb1(name, shape, dt=F):
            return sb(name, shape, dt, ssm)

        x_l = [sb1("x_l0", [128, CH[0], W]), sb1("x_l1", [128, 2 * CH[1], W // 2]), sb1("x_l2", [128, 2 * CH[2], W // 2])]
        w_ssm = sb1("w_ssm", [128, LAYERS, 3, 128])
        vecs = sb1("vecs", [128, LAYERS, 2])
        a_neg = sb1("a_neg", [128, LAYERS, D])
        sel_red = sb1("sel_red", [128, 16, 32])
        sel_bc = sb1("sel_bc", [96, 16, 128], BF)

        parts = sb1("parts", [96, 2, 4, 2, W], BF)
        bmat = sb1("bmat", [128, 2, W])
        cmat = sb1("cmat", [128, 2, W])
        z = sb1("z", [128, W])
        ez = sb1("ez", [128, W])
        az = ez
        lnz = sb1("lnz", [128, W])
        onepe = sb1("onepe", [128, W])
        rounded = onepe
        skip_w = sb1("skip_w", [128, LAYERS, 128])
        neg_id = sb1("neg_id", [128, 128], BF)
        relu_z = sb1("relu_z", [128, W])
        src = sb1("src", [128, 2, W])
        hi = sb1("hi", [128, 2, W], BF)
        mid = sb1("mid", [128, 2, W], BF)
        lo = sb1("lo", [128, 2, W], BF)
        RA, RH, RG = 8, 8, 8
        decay = sb1("decay", [128, RA, 2 * W])
        h = sb1("h", [128, RH, 2 * W])
        g = sb1("g", [128, RG, 2 * W])
        y_sb = sb1("y_sb", [128, W])

        ps_delta = ssm.enter_context(nc.psum_tensor("ps_delta", [128, 2, 512], F))
        ps_dx = ssm.enter_context(nc.psum_tensor("ps_dx", [128, 2, 2, 512], F))
        ps_y = ssm.enter_context(nc.psum_tensor("ps_y", [128, 512], F))
        ps_proj = ssm.enter_context(nc.psum_tensor("ps_proj", [128, 512], F))

        ssm.close()

        w_v = sb("w_v", [128, 2, 4, 256])
        normed = sb("normed", [128, HB, 32])
        h_att = sb("h_att", [128, HALF])
        res = sb("res", [128, HALF])
        cent = sb("cent", [128, HALF])
        sq = sb("sq", [128, HALF])
        lnvar = sb("lnvar", [128, HALF])
        rstd = sb("rstd", [128, HALF])
        eps_col = sb("eps_col", [128, 1])
        scores = sb("scores", [128, 2, BATCH, 32])
        scores_t = sb("scores_t", [128, 2, BATCH, 32])
        esum = sb("esum", [128, 2, BATCH])
        zeros = sb("zeros", [128, 512])
        qk = ExitStack()
        q_all = sb("q_all", [128, NHP, BATCH * T], F, qk)
        k_all = sb("k_all", [128, NHP, BATCH * T], F, qk)
        RD = 4
        diff = sb("diff", [128, RD, HALF], F, qk)
        dist = sb("dist", [128, RD, HALF], F, qk)
        qk.close()
        vals = ExitStack()
        v_all = sb("v_all", [128, BATCH, 2, 2, D], F, vals)
        sig = sb("sig", [128, 2, 512], F, vals)
        gated = sb("gated", [128, HB, 32], F, vals)
        vals.close()
        f_in = sb("f_in", [128, HALF])
        rh = sb("rh", [64, HALF])
        h1 = sb("h1", [128, NE // 2, 2, HALF])
        h2 = sb("h2", [128, NE // 2, 2, HALF])
        logit = sb("logit", [TT, 16, NE])
        prob = sb("prob", [TT, 16, NE])
        stat = sb("stat", [TT, 4, 16])
        beats = sb("beats", [TT, 2, 16, NE * NE])
        rank = sb("rank", [TT, 16, NE])
        gate = sb("gate", [TT, 16, NE])
        eo = sb("eo", [TT, 3, NE * D])
        mix = sb("mix", [TT, 16, D])
        fin = sb("fin", [TT, 16, D])
        P = ctx.enter_context(nc.psum_tensor("P", [128, 8, 512], F))

        x_first = sem("x_first")
        x_rest = sem("x_rest")
        proj_loaded = sem("proj_loaded")
        split_loaded = sem("split_loaded")
        a_loaded = sem("a_loaded")
        w_loaded = sem("w_loaded")
        a_exp = sem("a_exp")
        const_done = sem("const_done")
        delta_bcast = sem("delta_bcast")
        dx_bcast = sem("dx_bcast")
        exp_done = sem("exp_done")
        u_done = sem("u_done")
        scan_done = sem("scan_done")
        prod_done = sem("prod_done")
        reduce_done = sem("reduce_done")
        y_copy = sem("y_copy")
        pooled = sem("pooled")
        split_done = sem("split_done")
        decay_zero = sem("decay_zero")
        proj_done = sem("proj_done")
        proj_evac = sem("proj_evac")
        act_pre = sem("act_pre")
        step_size = sem("step_size")
        inputs_made = sem("inputs_made")
        parts_loaded = sem("parts_loaded")
        stored = sem("stored")
        weights_loaded = sem("weights_loaded")
        w_v_loaded = sem("w_v_loaded")
        h_ready = sem("h_ready")
        ln = {n: sem("ln_" + n) for n in ("mean", "cent", "sq", "var", "log", "rstd", "newton", "scaled", "out")}
        q_proj = sem("q_proj")
        q_ready = sem("q_ready")
        k_proj = sem("k_proj")
        k_ready = sem("k_ready")
        k_ready_act = sem("k_ready_act")
        diff_dve = sem("diff_dve")
        diff_pool = sem("diff_pool")
        dist_act = sem("dist_act")
        dist_dve = sem("dist_dve")
        dist_used = sem("dist_used")
        scores_exp = sem("scores_exp")
        pad_zero = sem("pad_zero")
        softmax = sem("softmax")
        v_proj = sem("v_proj")
        v_ready = sem("v_ready")
        o_done = sem("o_done")
        sig_done = sem("sig_done")
        gated_done = sem("gated_done")
        fan_done = sem("fan_done")
        att_done = sem("att_done")
        r1_done = sem("r1_done")
        rh_ready = sem("rh_ready")
        r2_done = sem("r2_done")
        route = sem("route")
        route_exp = sem("route_exp")
        e12_done = sem("e12_done")
        e12_relu = sem("e12_relu")
        e3_done = sem("e3_done")
        e3_used = sem("e3_used")
        gates_ready = sem("gates_ready")
        mixing = sem("mixing")
        mixed = sem("mixed")
        back = sem("back")
        final = sem("final")

        LAG = 7
        PRE = 9
        NDMA = 12 * 16

        A_Z, A_AZ, A_EZ, A_ONEPE, A_LNZ, A_RELU, A_ROUNDED, A_STEP, A_HI, A_MID0, A_LO0, A_MID1, A_LO1 = range(1, 14)
        PER_ACT = 13

        def wait(eng, s, v):
            if isinstance(v, int) and v <= 0:
                return
            eng.wait_ge(s, v)

        def flat(t3, l, c):
            return t3[:, c, :] if l == 0 else t3[:, :, :].rearrange("p (c two) n -> p c (two n)", two=2)[:, c, :]

        def schedule(eng, step):
            for l in range(LAYERS):
                last = CH[l] - 1
                step((l, 0, 0), None if l == 0 else (l - 1, CH[l - 1] - 1, 1), (l, 1, 1))
                if last - 1 > 2:
                    with eng.Fori(0, (last - 1) // 2) as pair:
                        c = pair * 2 + 1
                        step((l, c, 1), (l, c - 1, 0), (l, c + 1, 0))
                        step((l, c + 1, 0), (l, c, 1), (l, c + 2, 1))
                elif last > 1:
                    step((l, 1, 1), (l, 0, 0), (l, 2, 0))
                    step((l, 2, 0), (l, 1, 1), (l, 3, 1))
                step((l, last, 1), (l, last - 1, 0), (l + 1, 0, 0) if l + 1 < LAYERS else None)

        UPFRONT = 10
        TILES = [(hg, t, s, 2 * hg + hp) for hg in range(2) for t in range(T) for s in range(2) for hp in range(2)]
        BY_POOL = [i % 8 in (2, 5, 7) for i in range(len(TILES))]
        BY_DVE = [i % 16 in (1, 6, 11) for i in range(len(TILES))]
        made = [sum(1 for o in BY_POOL[:i + 1] if o == BY_POOL[i]) for i in range(len(TILES))]
        sized = [sum(1 for o in BY_DVE[:i + 1] if o == BY_DVE[i]) for i in range(len(TILES))]

        def wait_diff(eng, i):
            eng.wait_ge(diff_pool if BY_POOL[i] else diff_dve, made[i])

        def wait_dist(eng, i):
            if i >= 0:
                eng.wait_ge(dist_dve if BY_DVE[i] else dist_act, sized[i])

        LATER = [(mean_w, "mean_w"), (w_q, "w_q"), (b_q, "b_q"), (w_k, "w_k"), (sel_k, "sel_k"),
                 (b_v, "b_v"), (sel_key, "sel_key"), (key_rows, "key_rows"), (w_fan, "w_fan"), (b_fan, "b_fan"), (w_r1, "w_r1"),
                 (b_r1, "b_r1"), (w_r2, "w_r2"), (b_r2, "b_r2"), (lower, "lower"), (w_e1, "w_e1"), (b_e1, "b_e1"), (w_e2, "w_e2"),
                 (b_e2, "b_e2"), (w_e3, "w_e3"), (b_e3, "b_e3")]
        HIDDEN = [(s, c, layer, pair) for c in range(2) for s in range(2) for layer in range(2) for pair in range(NE // 2)]
        LAST = [(s, c, k, 2 * k + s) for c in range(2) for s in range(2) for k in range(4 * c, 4 * c + 4)]
        block = ctx.enter_context(nc.Block())

        def difference(engine, eng, i, tile):
            hg, t, s, hp = tile
            wait_dist(eng, i - RD)
            q = q_all[:, hp, s * HALF:(s + 1) * HALF].rearrange("p (b t) -> p b t", t=T)
            k = k_all[:, hp, s * HALF:(s + 1) * HALF].rearrange("p (b t) -> p b t", t=T)[:, :, t:t + 1].broadcast_to([128, HB, T])
            return engine.tensor_tensor(out=diff[:, i % RD, :].rearrange("p (b t) -> p b t", t=T), in0=q, in1=k, op=ALU.subtract)

        @block.sync
        def _(sp):
            sp.dma_start(x_l[0][:, 0, :], d["x"][:, 0:W]).then_inc(x_first, 16)
            sp.dma_start(w_ssm[:, 0, :, :], d["w_ssm"][:, 0, :, :]).then_inc(proj_loaded, 16)
            sp.dma_start(vecs[:], d["vecs"]).then_inc(proj_loaded, 16)
            sp.dma_start(neg_id[:], d["neg_id"]).then_inc(split_loaded, 16)
            sp.dma_start(ident[:], d["ident"]).then_inc(split_loaded, 16)
            sp.dma_start(a_neg[:], d["a_log"]).then_inc(a_loaded, 16)
            sp.dma_start(sel_bc[:], d["sel_bc"]).then_inc(w_loaded, 16)
            sp.dma_start(sel_red[:], d["sel_red"]).then_inc(w_loaded, 16)
            sp.dma_start(skip_w[:], d["skip_w"]).then_inc(w_loaded, 16)
            def load_parts(l, c, slot):
                k = BASE[l] + c
                wait(sp, dx_bcast, PAIRS * (k - 1))
                for i, (piece, n) in enumerate(((hi, A_HI), (mid, A_MID1), (lo, A_LO1))):
                    sp.wait_ge(act_pre, PER_ACT * k + n)
                    for j in range(4):
                        sp.dma_start(parts[32 * i:32 * i + 32, slot, j, :, 0:W], piece[32 * j:32 * j + 32, :, 0:W])\
                          .then_inc(parts_loaded, 16)

            load_parts(0, 0, 0)
            sp.dma_start(x_l[0][:, 1:CH[0], :], d["x"][:, W:].rearrange("p (c n) -> p c n", n=W)).then_inc(x_rest, 16)
            sp.dma_start(w_ssm[:, 1:LAYERS, :, :], d["w_ssm"][:, 1:LAYERS, :, :]).then_inc(x_rest, 16)
            for tile, name in LATER:
                sp.dma_start(tile[:], d[name]).then_inc(weights_loaded, 16)

            def step(chunk, prev, nxt):
                if nxt:
                    load_parts(*nxt)
            schedule(sp, step)
            sp.wait_ge(y_copy, NCH)
            sp.dma_start(w_v[:], d["w_v"]).then_inc(w_v_loaded, 16)
            sp.wait_ge(final, 1)
            sp.dma_start(out, fin[:]).then_inc(stored, 16)
            sp.wait_ge(stored, 16)

        @block.scalar
        def _(act):
            act.preload_act_table_set("natural_log_exp_and_others")

            def prelude(l, c, slot, part):
                k = BASE[l] + c
                def done(n):
                    act.wait_ge(act_pre, PER_ACT * k + n)

                if part == 0:
                    act.wait_ge(proj_done, 3 * k + 1)
                    nc.scalar.activation(z[:, 0:W], ps_proj[:, 0:W], ACT.Identity, bias=vecs[:, l, 1:2], scale=vecs[:, l, 0:1]).then_inc(act_pre, 1)
                    done(A_Z)
                    nc.scalar.activation(az[:, 0:W], z[:, 0:W], ACT.Abs).then_inc(act_pre, 1)
                elif part == 1:
                    done(A_AZ)
                    nc.scalar.activation(ez[:, 0:W], az[:, 0:W], ACT.Exp, scale=-1.0).then_inc(act_pre, 1)
                elif part == 2:
                    done(A_EZ)
                    nc.scalar.activation(onepe[:, 0:W], ez[:, 0:W], ACT.Identity, bias=1.0).then_inc(act_pre, 1)
                    nc.scalar.activation(lnz[:, 0:W], ez[:, 0:W], ACT.Ln, bias=1.0).then_inc(act_pre, 1)
                elif part == 3:
                    nc.scalar.activation(relu_z[:, 0:W], z[:, 0:W], ACT.Relu).then_inc(act_pre, 1)
                    done(A_ONEPE)
                    nc.scalar.activation(rounded[:, 0:W], onepe[:, 0:W], ACT.Identity, bias=1.0, scale=-1.0).then_inc(act_pre, 1)
                elif part == 4:
                    act.wait_ge(step_size, k + 1)
                    nc.scalar.activation(src[:, 0, 0:W], ps_proj[:, 0:W], ACT.Copy).then_inc(act_pre, 1)
                elif part == 5:
                    wait(act, parts_loaded, NDMA * k)
                    act.wait_ge(inputs_made, k + 1)
                    nc.scalar.activation(hi[:, :, 0:W], src[:, :, 0:W], ACT.Copy).then_inc(act_pre, 1)
                elif part == 6:
                    wait(act, u_done, PAIRS * (k - 1))
                    act.wait_ge(proj_done, 3 * k + 2)
                    nc.scalar.activation(bmat[:, slot, :], ps_proj[:, 0:W], ACT.Copy).then_inc(proj_evac, 1)
                elif part == 11:
                    wait(act, prod_done, PAIRS * (k - 1))
                    act.wait_ge(proj_done, 3 * k + 3)
                    nc.scalar.activation(cmat[:, slot, :], ps_proj[:, 0:W], ACT.Copy).then_inc(proj_evac, 1)
                else:
                    which, third = (part - 7) // 2, (part - 7) % 2
                    act.wait_ge(split_done, 4 * k + part - 6)
                    nc.scalar.activation((lo if third else mid)[:, which, 0:W], ps_proj[:, 0:W], ACT.Copy).then_inc(act_pre, 1)

            def finish(l, c, slot):
                k = BASE[l] + c
                act.wait_ge(reduce_done, PAIRS * (k + 1))
                if l < 2:
                    if not (isinstance(k, int) and k == 0):
                        act.wait_ge(pooled, k)
                    nc.scalar.activation(y_sb[:, 0:W], ps_y[:, 0:W], ACT.Copy, scale=0.5).then_inc(y_copy, 1)
                else:
                    nc.scalar.activation(h_tok[:, c * W:(c + 1) * W], ps_y[:, 0:W], ACT.Copy).then_inc(y_copy, 1)

            AT = {PRE + 1: 0, PRE + 2: 1, PRE + 3: 2, PRE + 4: 3, PRE + 7: 4, PRE + 9: 5, PRE + 10: 6, PRE + 12: 7, PRE + 14: 8, PRE + 17: 9, PRE + 19: 10,
                  PRE + 22: 11}
            act.wait_ge(proj_loaded, 32)
            for part in range(12):
                prelude(0, 0, 0, part)
                if part == 3:
                    act.wait_ge(const_done, 1)
                    nc.scalar.activation(a_neg[:], a_neg[:], ACT.Exp).then_inc(a_exp, 1)

            def step(chunk, prev, nxt):
                l, c, slot = chunk
                k = BASE[l] + c
                if isinstance(c, int) and c == 0:
                    act.wait_ge(decay_zero, l + 1)
                for q in range(PAIRS):
                    G = PAIRS * k + q
                    wait(act, scan_done, G - RA + 1)
                    for r in range(2):
                        j = (2 * q + r) % 4
                        act.wait_ge(delta_bcast, 2 * G + r + 1)
                        e = 16 * j + q // 2
                        dst = decay[:, q % RA, r * W:(r + 1) * W].rearrange("p (b t) -> p b t", t=LEN[l])
                        s = ps_delta[:, r, 0:W].rearrange("p (b t) -> p b t", t=LEN[l])
                        nc.scalar.activation(dst[:, :, 1:], s[:, :, 1:], ACT.Exp, scale=a_neg[:, l, e:e + 1]).then_inc(exp_done, 1)
                    if prev and q == LAG:
                        finish(*prev)
                    if nxt and q in AT:
                        prelude(*nxt, AT[q])
            act.wait_ge(const_done, 2)
            schedule(act, step)
            finish(LAYERS - 1, CH[-1] - 1, 1)
            act.wait_ge(weights_loaded, 16 * len(LATER))

            def norm(n):
                for c in range(2):
                    cols = slice(c * COLS, (c + 1) * COLS)
                    act.wait_ge(ln["cent"], 2 * n + c + 1)
                    nc.scalar.activation(sq[:, cols], cent[:, cols], ACT.Square).then_inc(ln["sq"], 1)
                for c in range(2):
                    cols = slice(c * COLS, (c + 1) * COLS)
                    act.wait_ge(ln["var"], 2 * n + c + 1)
                    nc.scalar.activation(lnvar[:, cols], P[:, 2 + c, 0:COLS], ACT.Ln, bias=eps_col[:, 0:1]).then_inc(ln["log"], 1)
                    act.wait_ge(ln["log"], 2 * n + c + 1)
                    nc.scalar.activation(rstd[:, cols], lnvar[:, cols], ACT.Exp, scale=-0.5).then_inc(ln["rstd"], 1)

            act.wait_ge(pad_zero, 1)
            norm(0)

            def query(i):
                hp, s, c = i // 4, i // 2 % 2, i % 2
                act.wait_ge(q_proj, i + 1)
                nc.scalar.activation(q_all[:, hp, s * HALF + c * COLS:s * HALF + (c + 1) * COLS], P[:, 4 + i % 4, 0:COLS], ACT.Identity,
                                     bias=b_q[:, hp:hp + 1]).then_inc(q_ready, 1)

            for i in range(8):
                query(i)
                if i % 2:
                    hp = NHP - 1
                    k_cols = (0, 2, 1, 3)[i // 2]
                    act.wait_ge(k_ready, 3 * (i // 2 + 1))
                    nc.scalar.activation(k_all[:, hp, k_cols * COLS:(k_cols + 1) * COLS], P[:, k_cols, 0:COLS], ACT.Copy, scale=w_k[:, hp:hp + 1]).then_inc(k_ready_act, 1)
            for i in range(8, UPFRONT):
                query(i)

            def exps(hg):
                act.wait_ge(dist_used, len(TILES) // 2 * (hg + 1))
                act.wait_ge(pad_zero, 2)
                for i in range(4):
                    s, c = i // 2, i % 2
                    nc.scalar.activation(scores[:, hg, 32 * s + 16 * c:32 * s + 16 * c + 16, 0:T],
                                         P[:, 4 * hg + i, 0:COLS].rearrange("p (b t) -> p b t", t=T), ACT.Exp, scale=-0.125).then_inc(scores_exp, 1)

            for i in range(len(TILES)):
                if not BY_DVE[i]:
                    wait_diff(act, i)
                    wait(act, dist_used, i - RD + 1)
                    nc.scalar.activation(dist[:, i % RD, :], diff[:, i % RD, :], ACT.Abs).then_inc(dist_act, 1)
                if i % 4 == 2 and 0 <= i // 4 - 1 < 16 - UPFRONT:
                    query(UPFRONT + i // 4 - 1)
                if i == len(TILES) // 2 + 8:
                    exps(0)
            exps(1)
            for c in range(2):
                act.wait_ge(o_done, c + 1)
                nc.scalar.activation(sig[:, c, :], P[:, 4 + c, :], ACT.Sigmoid, scale=1.702).then_inc(sig_done, 1)
            act.preload_act_table_set("natural_log_exp_and_others")
            norm(1)
            for i, (s, c, layer, pair) in enumerate(HIDDEN):
                if i in (3, 4):
                    act.wait_ge(r1_done, i - 2)
                    nc.scalar.activation(rh[:, (i - 3) * COLS:(i - 2) * COLS], P[0:64, 1 + i, 0:COLS], ACT.Relu, bias=b_r1[:, 0:1]).then_inc(rh_ready, 1)
                if i == 7:
                    act.wait_ge(route, 3)
                    nc.scalar.activation(prob[:], logit[:], ACT.Exp).then_inc(route_exp, 1)
                if i == 9:
                    act.wait_ge(route, 6)
                    nc.scalar.activation(gate[:], prob[:], ACT.Exp).then_inc(route_exp, 1)
                act.wait_ge(e12_done, i + 1)
                nc.scalar.activation((h2 if layer else h1)[:, pair, s, c * COLS:(c + 1) * COLS], P[:, i % 4, 0:COLS], ACT.Relu,
                                     bias=(b_e2 if layer else b_e1)[:, pair:pair + 1]).then_inc(e12_relu, 1)

        @block.vector
        def _(dve):
            dve.wait_ge(a_loaded, 16)
            nc.vector.tensor_scalar(out=a_neg[:], in0=a_neg[:], scalar1=80.0, scalar2=None, op0=ALU.min).then_inc(const_done, 1)

            def prelude(l, c, slot):
                k = BASE[l] + c
                dve.wait_ge(act_pre, PER_ACT * k + A_STEP)
                nc.vector.tensor_tensor(out=src[:, 1, 0:W], in0=src[:, 0, 0:W], in1=flat(x_l[l], l, c), op=ALU.mult).then_inc(inputs_made, 1)

            dve.wait_ge(x_first, 16)
            prelude(0, 0, 0)
            dve.wait_ge(a_exp, 1)
            nc.vector.tensor_scalar(out=a_neg[:], in0=a_neg[:], scalar1=-1.0, scalar2=None, op0=ALU.mult).then_inc(const_done, 1)

            def finish(l, c, slot):
                if l < 2:
                    k = BASE[l] + c
                    dve.wait_ge(y_copy, k + 1)
                    pairs = y_sb[:, 0:W].rearrange("p (b t) -> p b t", t=LEN[l])[:, :, 0:2 * LEN[l + 1]].rearrange("p b (t two) -> p b t two", two=2)
                    dst = x_l[l + 1][:, c, :].rearrange("p (b t) -> p b t", t=LEN[l + 1])
                    nc.vector.tensor_tensor(out=dst, in0=pairs[:, :, :, 0], in1=pairs[:, :, :, 1], op=ALU.add).then_inc(pooled, 1)

            def inputs(l, k, slot, q):
                G = PAIRS * k + q
                dve.wait_ge(dx_bcast, G + 1)
                wait(dve, prod_done, G - RH + 1)
                dst = h[:, q % RH, :].rearrange("p (r n) -> p r n", r=2)
                nc.vector.tensor_tensor(out=dst, in0=ps_dx[:, q % 2, :, 0:W], in1=bmat[:, slot, :].unsqueeze(1).broadcast_to([128, 2, W]), op=ALU.mult)\
                  .then_inc(u_done, 1)

            def step(chunk, prev, nxt):
                l, c, slot = chunk
                k = BASE[l] + c
                if isinstance(c, int) and c == 0:
                    wait(dve, scan_done, PAIRS * k)
                    for a in range(RA):
                        dst = decay[:, a, :].rearrange("p (b t) -> p b t", t=LEN[l])[:, :, 0:1]
                        last = nc.vector.memset(dst, 0.0)
                    last.then_inc(decay_zero, 1)
                dve.wait_ge(proj_evac, 2 * k + 1)
                inputs(l, k, slot, 0)
                for q in range(PAIRS):
                    G = PAIRS * k + q
                    if q + 1 < PAIRS:
                        inputs(l, k, slot, q + 1)
                    dve.wait_ge(u_done, G + 1)
                    dve.wait_ge(exp_done, 2 * G + 2)
                    nc.vector.tensor_tensor_scan(out=h[:, q % RH, :], data0=decay[:, q % RA, :], data1=h[:, q % RH, :],
                                                 initial=0.0, op0=ALU.mult, op1=ALU.add).then_inc(scan_done, 1)
                    if prev and q == LAG:
                        finish(*prev)
                    if isinstance(k, int) and k == 0 and q == PRE:
                        dve.wait_ge(x_rest, 32)
                    if nxt and q == PRE + 7:
                        prelude(*nxt)
            schedule(dve, step)
            dve.wait_ge(weights_loaded, 16 * len(LATER))

            def norm(n, x, dst):
                for c in range(2):
                    cols = slice(c * COLS, (c + 1) * COLS)
                    dve.wait_ge(ln["mean"], 2 * n + c + 1)
                    nc.vector.tensor_tensor(out=cent[:, cols], in0=x[:, cols], in1=P[:, c, 0:COLS], op=ALU.subtract).then_inc(ln["cent"], 1)
                for c in range(2):
                    cols = slice(c * COLS, (c + 1) * COLS)
                    dve.wait_ge(ln["rstd"], 2 * n + c + 1)
                    nc.vector.scalar_tensor_tensor(out=sq[:, cols], in0=P[:, 2 + c, 0:COLS], scalar=EPS, in1=rstd[:, cols], op0=ALU.add, op1=ALU.mult).then_inc(ln["newton"], 1)
                    dve.wait_ge(ln["newton"], 4 * n + 2 * c + 1)
                    nc.vector.scalar_tensor_tensor(out=sq[:, cols], in0=sq[:, cols], scalar=-0.5, in1=rstd[:, cols], op0=ALU.mult, op1=ALU.mult).then_inc(ln["newton"], 1)
                    dve.wait_ge(ln["newton"], 4 * n + 2 * c + 2)
                    dve.wait_ge(ln["scaled"], 2 * n + c + 1)
                    nc.vector.scalar_tensor_tensor(out=dst(c), in0=sq[:, cols].rearrange("p (b t) -> p b t", t=T), scalar=1.5,
                                                   in1=cent[:, cols].rearrange("p (b t) -> p b t", t=T), op0=ALU.add, op1=ALU.mult).then_inc(ln["out"], 1)

            dve.wait_ge(y_copy, NCH)
            dve.wait_ge(reduce_done, PAIRS * NCH)
            nc.vector.memset(eps_col[:], EPS)
            nc.vector.memset(normed[:, :, T:32], 0.0).then_inc(pad_zero, 1)
            nc.vector.memset(scores[:, :, :, T:32], 0.0).then_inc(pad_zero, 1)
            nc.vector.memset(zeros[:], 0.0).then_inc(pad_zero, 1)
            norm(0, h_tok, lambda c: normed[:, 16 * c:16 * c + 16, 0:T])
            for n, i in enumerate((0, 2, 1, 3)):
                dve.wait_ge(k_proj, n + 1)
                for hp in range(NHP - 1):
                    nc.vector.tensor_scalar(out=k_all[:, hp, i * COLS:(i + 1) * COLS], in0=P[:, i, 0:COLS], scalar1=w_k[:, hp:hp + 1], scalar2=None,
                                            op0=ALU.mult).then_inc(k_ready, 1)
            dve.wait_ge(k_ready, 12)
            dve.wait_ge(q_ready, 8)

            def soft(hg, n):
                sc = scores[:, hg, :, :]
                if n == 0:
                    dve.wait_ge(scores_exp, 4 * (hg + 1))
                    ins = nc.vector.reduce_sum(esum[:, hg, :], sc, AX.X)
                else:
                    dve.wait_ge(softmax, 6 * hg + n)
                if n == 1:
                    ins = nc.vector.tensor_scalar(out=esum[:, hg, :], in0=esum[:, hg, :], scalar1=1.0, scalar2=None, op0=ALU.add)
                elif n == 2:
                    ins = nc.vector.reciprocal(esum[:, hg, :], esum[:, hg, :])
                elif n == 3:
                    ins = nc.vector.tensor_scalar(out=esum[:, hg, :], in0=esum[:, hg, :], scalar1=key_rows[:, 0:1], scalar2=None, op0=ALU.mult)
                elif n == 4:
                    ins = nc.vector.tensor_tensor(out=sc, in0=sc, in1=esum[:, hg, :].unsqueeze(2).broadcast_to([128, BATCH, 32]), op=ALU.mult)
                elif n == 5:
                    ins = nc.vector.transpose(scores_t[:, hg, :, :].rearrange("p b t -> p (b t)"), sc.rearrange("p b t -> p (b t)"))
                ins.then_inc(softmax, 1)

            def size(i):
                if i >= 0 and BY_DVE[i]:
                    wait_diff(dve, i)
                    wait(dve, dist_used, i - RD + 1)
                    nc.vector.tensor_scalar(out=dist[:, i % RD, :].bitcast(U32), in0=diff[:, i % RD, :].bitcast(U32), scalar1=0x7FFFFFFF, scalar2=None,
                                            op0=ALU.bitwise_and).then_inc(dist_dve, 1)

            for i, tile in enumerate(TILES):
                if i == len(TILES) // 2:
                    dve.wait_ge(q_ready, 16)
                    dve.wait_ge(k_ready_act, 4)
                if not BY_POOL[i]:
                    difference(nc.vector, dve, i, tile).then_inc(diff_dve, 1)
                size(i - 1)
                if i in range(len(TILES) // 2 + 24, len(TILES) // 2 + 30):
                    soft(0, i - len(TILES) // 2 - 24)
            size(len(TILES) - 1)
            for i in range(32):
                if i % 2 and i < 12:
                    soft(1, i // 2)
                dve.wait_ge(v_proj, i + 1)
                nc.vector.tensor_tensor(out=v_all[:, 2 * i:2 * i + 2, :, :, :].rearrange("p b f g w -> p b (f g w)"), in0=P[:, i % 4, :].rearrange("p (b n) -> p b n", b=2),
                                        in1=b_v[:, :].unsqueeze(1).broadcast_to([128, 2, 256]), op=ALU.add).then_inc(v_ready, 1)
            for c in range(2):
                dve.wait_ge(sig_done, c + 1)
                nc.vector.tensor_tensor(out=gated[:, 16 * c:16 * c + 16, :].rearrange("p b t -> p (b t)"), in0=P[:, 4 + c, :], in1=sig[:, c, :], op=ALU.mult).then_inc(gated_done, 1)
            dve.wait_ge(h_ready, 1)
            for c in range(2):
                cols = slice(c * COLS, (c + 1) * COLS)
                dve.wait_ge(fan_done, c + 1)
                nc.vector.scalar_tensor_tensor(out=h_att[:, cols], in0=P[:, 6 + c, 0:COLS], scalar=b_fan[:, 0:1], in1=res[:, cols], op0=ALU.add, op1=ALU.add).then_inc(att_done, 1)
            dve.wait_ge(att_done, 2)
            norm(1, h_att, lambda c: f_in[:, c * COLS:(c + 1) * COLS].rearrange("p (b t) -> p b t", t=T))

            link = [0]

            def chained(ins):
                link[0] += 1
                ins.then_inc(route, 1)
                dve.wait_ge(route, link[0])

            def per_expert(v):
                return v.unsqueeze(2).broadcast_to([TT, 16, NE])

            dve.wait_ge(r2_done, 1)
            chained(nc.vector.tensor_tensor(out=logit[:], in0=P[0:TT, 7, 0:96].rearrange("p (k e) -> p k e", e=NE),
                                            in1=b_r2[:, :].unsqueeze(1).broadcast_to([TT, 16, NE]), op=ALU.add))
            chained(nc.vector.reduce_max(stat[:, 0, :], logit[:], AX.X))
            chained(nc.vector.tensor_tensor(out=logit[:], in0=logit[:], in1=per_expert(stat[:, 0, :]), op=ALU.subtract))
            dve.wait_ge(route_exp, 1)
            chained(nc.vector.reduce_sum(stat[:, 1, :], prob[:], AX.X))
            chained(nc.vector.reciprocal(stat[:, 2, :], stat[:, 1, :]))
            chained(nc.vector.tensor_tensor(out=prob[:], in0=prob[:], in1=per_expert(stat[:, 2, :]), op=ALU.mult))
            for n, op in ((0, ALU.is_ge), (1, ALU.is_gt)):
                for e in range(NE):
                    chained(nc.vector.tensor_tensor(out=beats[:, n, :, e * NE:(e + 1) * NE], in0=prob[:], in1=prob[:, :, e:e + 1].broadcast_to([TT, 16, NE]), op=op))
                chained(nc.vector.tensor_tensor(out=beats[:, n, :, :], in0=beats[:, n, :, :], in1=lower[:, n, :, :].rearrange("p a b -> p (a b)").unsqueeze(1).broadcast_to([TT, 16, NE * NE]), op=ALU.mult))
            chained(nc.vector.tensor_tensor(out=beats[:, 0, :, :], in0=beats[:, 0, :, :], in1=beats[:, 1, :, :], op=ALU.add))
            chained(nc.vector.reduce_sum(rank[:].rearrange("p k e -> p (k e)"), beats[:, 0, :, :].rearrange("p k (i j) -> p (k i) j", j=NE), AX.X))
            chained(nc.vector.tensor_scalar(out=rank[:], in0=rank[:], scalar1=2.0, scalar2=None, op0=ALU.is_lt))
            dve.wait_ge(route_exp, 2)
            chained(nc.vector.tensor_tensor(out=gate[:], in0=gate[:], in1=rank[:], op=ALU.mult))
            chained(nc.vector.reduce_sum(stat[:, 3, :], gate[:], AX.X))
            chained(nc.vector.reciprocal(stat[:, 0, :], stat[:, 3, :]))
            nc.vector.tensor_tensor(out=gate[:], in0=gate[:], in1=per_expert(stat[:, 0, :]), op=ALU.mult).then_inc(gates_ready, 1)

            def collect(i):
                dve.wait_ge(mixing, i + 1)
                nc.vector.reduce_sum(mix[:, LAST[i][3], :], eo[:, i % 3, :].rearrange("p (e o) -> p o e", e=NE), AX.X).then_inc(mixed, 1)

            for i in range(16):
                dve.wait_ge(e3_done, i + 1)
                wait(dve, mixed, i - 2)
                nc.vector.tensor_tensor(out=eo[:, i % 3, :], in0=P[0:TT, 4 + i % 3, 0:NE * D], in1=b_e3[:], op=ALU.add).then_inc(e3_used, 1)
                if i > 1:
                    collect(i - 2)
            collect(14)
            collect(15)
            dve.wait_ge(back, 8)
            dve.wait_ge(mixed, 16)
            for c in range(2):
                for s in range(2):
                    def tiles(t3):
                        return t3[:, 8 * c:8 * c + 8, :].rearrange("p (k s) (j l) -> p s k j l", s=2, j=4)[:, s, :, :, :]
                    last = nc.vector.tensor_tensor(out=tiles(fin), in0=tiles(mix), in1=P[0:TT, c, :].rearrange("p (k j s l) -> p s k j l", k=4, j=4, s=2)[:, s, :, :, :], op=ALU.add)
            last.then_inc(final, 1)

        @block.gpsimd
        def _(pool):
            def step(chunk, prev, nxt):
                l, c, slot = chunk
                k = BASE[l] + c
                pool.wait_ge(proj_evac, 2 * k + 2)
                for q in range(PAIRS):
                    G = PAIRS * k + q
                    pool.wait_ge(scan_done, G + 1)
                    wait(pool, reduce_done, G - RG + 1)
                    nc.gpsimd.tensor_tensor(out=g[:, q % RG, :].rearrange("p (r n) -> p r n", r=2), in0=h[:, q % RH, :].rearrange("p (r n) -> p r n", r=2),
                                            in1=cmat[:, slot, :].unsqueeze(1).broadcast_to([128, 2, W]), op=ALU.mult).then_inc(prod_done, 1)
            schedule(pool, step)

            def norm(n):
                for c in range(2):
                    cols = slice(c * COLS, (c + 1) * COLS)
                    pool.wait_ge(ln["rstd"], 2 * n + c + 1)
                    nc.gpsimd.tensor_tensor(out=cent[:, cols], in0=cent[:, cols], in1=rstd[:, cols], op=ALU.mult).then_inc(ln["scaled"], 1)

            norm(0)
            pool.wait_ge(ln["out"], 2)
            nc.gpsimd.tensor_tensor(out=res[:, :].rearrange("p (b t) -> p b t", t=T), in0=h_tok[:, :].rearrange("p (b t) -> p b t", t=T),
                                    in1=normed[:, :, 0:T], op=ALU.add).then_inc(h_ready, 1)
            pool.wait_ge(k_ready, 12)
            pool.wait_ge(q_ready, 8)
            for i, tile in enumerate(TILES):
                if i == len(TILES) // 2:
                    pool.wait_ge(q_ready, 16)
                    pool.wait_ge(k_ready_act, 4)
                if BY_POOL[i]:
                    difference(nc.gpsimd, pool, i, tile).then_inc(diff_pool, 1)
            norm(1)
            pool.wait_ge(gates_ready, 1)
            for i in range(16):
                pool.wait_ge(e3_used, i + 1)
                v = eo[:, i % 3, :].rearrange("p (e o) -> p e o", e=NE)
                nc.gpsimd.tensor_tensor(out=v, in0=v, in1=gate[:, LAST[i][3], :].unsqueeze(2).broadcast_to([TT, NE, D]), op=ALU.mult).then_inc(mixing, 1)

        @block.tensor
        def _(pe):
            pe.wait_ge(proj_loaded, 32)
            pe.wait_ge(x_first, 16)

            HALVES = (slice(0, W // 2), slice(W // 2, W))
            SOFTPLUS = {"e": (ez, A_EZ), "rounded": (rounded, A_ROUNDED), "log": (lnz, A_LNZ), "max": (relu_z, A_RELU)}

            def project(l, c, slot, part, half):
                k = BASE[l] + c
                cols = HALVES[half]
                if part in (0, 2, 7):
                    if part == 0:
                        if l > 0:
                            pe.wait_ge(pooled, BASE[l - 1] + 2 * c + 2)
                        wait(pe, proj_evac, 2 * k)
                    elif part == 2:
                        pe.wait_ge(act_pre, PER_ACT * k + A_STEP)
                    else:
                        pe.wait_ge(act_pre, PER_ACT * k + A_LO1)
                    last = nc.tensor.matmul(ps_proj[:, cols], w_ssm[:, l, {0: 2, 2: 0, 7: 1}[part], :], flat(x_l[l], l, c)[:, cols], start=True, stop=True)
                    if half:
                        last.then_inc(proj_done, 1)
                elif part in SOFTPLUS:
                    term, made = SOFTPLUS[part]
                    pe.wait_ge(act_pre, PER_ACT * k + made)
                    for n, cols in enumerate(HALVES):
                        last = nc.tensor.matmul(ps_proj[:, cols], ident[:], term[:, cols], start=(part == "e" and n == 0), stop=(part == "max"), skip_group_check=True)
                    if part == "max":
                        last.then_inc(step_size, 1)
                elif part in (3, 5):
                    which = (part - 3) // 2
                    pe.wait_ge(act_pre, PER_ACT * k + (A_LO0 if which else A_HI))
                    pe.wait_ge(proj_evac, 2 * k + 1)
                    nc.tensor.matmul(ps_proj[:, cols], ident[:], src[:, which, cols], start=(half == 0), stop=False, skip_group_check=True)
                    last = nc.tensor.matmul(ps_proj[:, cols], neg_id[:], hi[:, which, cols], start=False, stop=True, skip_group_check=True)
                    if half:
                        last.then_inc(split_done, 1)
                elif half:
                    which = (part - 4) // 2
                    pe.wait_ge(act_pre, PER_ACT * k + (A_MID1 if which else A_MID0))
                    for cols in HALVES:
                        last = nc.tensor.matmul(ps_proj[:, cols], neg_id[:], mid[:, which, cols], start=False, stop=True, skip_group_check=True)
                    last.then_inc(split_done, 1)

            for part in (0, "e", "rounded", "log", "max", 2, 3, 4, 5, 6, 7):
                if part == "e":
                    pe.wait_ge(split_loaded, 32)
                for half in ((1,) if part in SOFTPLUS else (0, 1)):
                    project(0, 0, 0, part, half)
            pe.wait_ge(w_loaded, 48)

            def reduce(l, c, slot, q):
                pe.wait_ge(prod_done, PAIRS * (BASE[l] + c) + q + 1)
                if q < 2:
                    if q == 0:
                        wait(pe, y_copy, BASE[l] + c)
                    cols = HALVES[q]
                    nc.tensor.matmul(ps_y[:, cols], skip_w[:, l, :], flat(x_l[l], l, c)[:, cols], start=(q == 0), stop=False, skip_group_check=True)
                for r in range(2):
                    j = (2 * q + r) % 4
                    last = nc.tensor.matmul(ps_y[32 * j:32 * j + 32, 0:W], sel_red[:, q // 2, :], g[:, q % RG, r * W:(r + 1) * W],
                                            start=False, stop=(q // 2 == 15), tile_position=(0, 32 * j), skip_group_check=True)
                last.then_inc(reduce_done, 1)

            AT = {PRE: (0, 0), PRE + 1: (0, 1), PRE + 3: ("e", 1), PRE + 5: ("rounded", 1), PRE + 6: ("log", 1), PRE + 7: ("max", 1), PRE + 8: (2, 0),
                  PRE + 9: (2, 1), PRE + 11: (3, 0), PRE + 12: (3, 1), PRE + 13: (4, 1), PRE + 15: (5, 0), PRE + 16: (5, 1), PRE + 18: (6, 1),
                  PRE + 20: (7, 0), PRE + 21: (7, 1)}

            def step(chunk, prev, nxt):
                l, c, slot = chunk
                k = BASE[l] + c
                pe.wait_ge(parts_loaded, NDMA * (k + 1))
                for q in range(PAIRS):
                    if isinstance(k, int) and k == 0 and q == PRE:
                        pe.wait_ge(x_rest, 32)
                    G = PAIRS * k + q
                    el = q // 2
                    wait(pe, u_done, G - 1)
                    for r in range(2):
                        last = nc.tensor.matmul(ps_dx[:, q % 2, r, 0:W], sel_bc[:, el, :], parts[:, slot, (2 * q + r) % 4, 1, :], start=True, stop=True)
                    last.then_inc(dx_bcast, 1)
                    for r in range(2):
                        wait(pe, exp_done, 2 * G + r - 1)
                        nc.tensor.matmul(ps_delta[:, r, 0:W], sel_bc[:, el, :], parts[:, slot, (2 * q + r) % 4, 0, :], start=True, stop=True).then_inc(delta_bcast, 1)
                    if q >= LAG:
                        reduce(l, c, slot, q - LAG)
                    elif prev:
                        reduce(*prev, PAIRS - LAG + q)
                    if nxt and q in AT:
                        project(*nxt, *AT[q])
            schedule(pe, step)
            for q in range(PAIRS - LAG, PAIRS):
                reduce(LAYERS - 1, CH[-1] - 1, 1, q)
            pe.wait_ge(weights_loaded, 16 * len(LATER))

            def norm(n, x, ready, count):
                for c in range(2):
                    pe.wait_ge(ready, count)
                    nc.tensor.matmul(P[:, c, 0:COLS], mean_w[:], x[:, c * COLS:(c + 1) * COLS], start=True, stop=True).then_inc(ln["mean"], 1)
                for c in range(2):
                    pe.wait_ge(ln["sq"], 2 * n + c + 1)
                    nc.tensor.matmul(P[:, 2 + c, 0:COLS], mean_w[:], sq[:, c * COLS:(c + 1) * COLS], start=True, stop=True).then_inc(ln["var"], 1)

            norm(0, h_tok, y_copy, NCH)
            for i, (c, s) in enumerate(((0, 0), (0, 1), (1, 0), (1, 1))):
                pe.wait_ge(ln["out"], c + 1)
                nc.tensor.matmul(P[:, 2 * s + c, 0:COLS], sel_k[:, s, :], normed[:, 16 * c:16 * c + 16, 0:T], start=True, stop=True).then_inc(k_proj, 1)

            def query(i):
                hp, s, c = i // 4, i // 2 % 2, i % 2
                wait(pe, q_ready, i - 3)
                nc.tensor.matmul(P[:, 4 + i % 4, 0:COLS], w_q[:, s, hp, :], normed[:, 16 * c:16 * c + 16, 0:T], start=True, stop=True).then_inc(q_proj, 1)

            for i in range(UPFRONT):
                query(i)
            pe.wait_ge(k_ready, 12)
            pe.wait_ge(k_ready_act, 4)
            for i, (hg, t, s, hp) in enumerate(TILES):
                if i == len(TILES) // 2:
                    pe.wait_ge(q_ready, 16)
                wait_dist(pe, i)
                lo_row = 64 * (hp % 2)
                for c in range(2):
                    last = nc.tensor.matmul(P[lo_row:lo_row + 64, 4 * hg + 2 * s + c, 0:COLS], sel_key[:, t, :], dist[:, i % RD, c * COLS:(c + 1) * COLS],
                                            start=(t == 0), stop=(t == T - 1), tile_position=(0, lo_row))
                last.then_inc(dist_used, 1)
                if i % 4 == 3 and i // 4 < 16 - UPFRONT:
                    query(UPFRONT + i // 4)
            def attend(hg, i):
                for b in (2 * i, 2 * i + 1):
                    s, b32 = b // HB, b % HB
                    for f in range(2):
                        last = nc.tensor.matmul(P[64 * s:64 * s + 64, 4 + b32 // 16, 32 * (b32 % 16):32 * (b32 % 16) + 32], v_all[:, b, f, hg, :],
                                                (scores if f else scores_t)[:, hg, b, :], start=False, stop=(hg == 1 and f == 1), tile_position=(0, 64 * s),
                                                skip_group_check=True)
                return last

            AHEAD = 4
            pe.wait_ge(w_v_loaded, 16)
            pe.wait_ge(pad_zero, 1)
            pe.wait_ge(scores_exp, 4)
            for i in range(32):
                wait(pe, v_ready, i - 3)
                for b in (2 * i, 2 * i + 1):
                    for h4 in range(4):
                        last = nc.tensor.matmul(P[32 * h4:32 * h4 + 32, i % 4, 256 * (b % 2):256 * (b % 2) + 256], normed[:, b % HB, :], w_v[:, b // HB, h4, :],
                                                start=True, stop=True, tile_position=(0, 32 * h4))
                last.then_inc(v_proj, 1)
                if i == AHEAD:
                    pe.wait_ge(pad_zero, 3)
                    pe.wait_ge(scores_exp, 8)
                    pe.wait_ge(softmax, 6)
                    for c in range(2):
                        nc.tensor.matmul(P[:, 4 + c, :], ident[:], zeros[:], start=True, stop=False, skip_group_check=True)
                if i >= AHEAD:
                    attend(0, i - AHEAD)
                if i == 16:
                    pe.wait_ge(softmax, 12)
                if i >= 16:
                    attend(1, i - 16)
            for i in range(16, 24):
                last = attend(1, i)
            last.then_inc(o_done, 1)
            pe.wait_ge(v_ready, 32)
            for i in range(32 - AHEAD, 32):
                attend(0, i)
            for i in range(24, 32):
                last = attend(1, i)
            last.then_inc(o_done, 1)
            for c in range(2):
                pe.wait_ge(gated_done, c + 1)
                nc.tensor.matmul(P[:, 6 + c, 0:COLS], w_fan[:], gated[:, 16 * c:16 * c + 16, 0:T], start=True, stop=True).then_inc(fan_done, 1)
            norm(1, h_att, att_done, 2)
            BEHIND = 11

            def last_layer(i):
                s, c, k, _ = LAST[i]
                pe.wait_ge(e12_relu, 6 * (i // 4 + 1))
                wait(pe, e3_used, i - 2)
                for pair in range(NE // 2):
                    last = nc.tensor.matmul(P[0:TT, 4 + i % 3, 128 * pair:128 * pair + 128], h2[:, pair, s, TT * k:TT * (k + 1)], w_e3[:, pair, :], start=True, stop=True)
                last.then_inc(e3_done, 1)

            pe.wait_ge(ln["out"], 3)
            for i, (s, c, layer, pair) in enumerate(HIDDEN):
                if i == 3:
                    pe.wait_ge(ln["out"], 4)
                    for n in range(2):
                        nc.tensor.matmul(P[0:64, 4 + n, 0:COLS], w_r1[:], f_in[:, n * COLS:(n + 1) * COLS], start=True, stop=True).then_inc(r1_done, 1)
                if i == 5:
                    pe.wait_ge(rh_ready, 2)
                    for k in range(8):
                        last = nc.tensor.matmul(P[0:TT, 7, 2 * NE * k:2 * NE * (k + 1)], rh[:, TT * k:TT * (k + 1)], w_r2[:], start=True, stop=True)
                    last.then_inc(r2_done, 1)
                cols = slice(c * COLS, (c + 1) * COLS)
                wait(pe, e12_relu, i - 2 if layer else i - 3)
                nc.tensor.matmul(P[:, i % 4, 0:COLS], w_e2[:, pair, :] if layer else w_e1[:, s, pair, :], h1[:, pair, s, cols] if layer else f_in[:, cols],
                                 start=True, stop=True).then_inc(e12_done, 1)
                if 0 <= i - BEHIND < 12:
                    last_layer(i - BEHIND)
            for n in range(12, 16):
                last_layer(n)
            for k in range(8):
                nc.tensor.transpose(P[0:TT, k // 4, 128 * (k % 4):128 * (k % 4) + 128], h_att[:, TT * k:TT * (k + 1)], ident[:]).then_inc(back, 1)


def lay_out(i):
    f = np.float32
    e = np.arange(D)
    def chan(a):
        a = np.asarray(a)
        return np.repeat(a.reshape(4, 1, 16, *a.shape[1:]), 2, axis=1).reshape(128, *a.shape[1:])
    half_of = np.repeat(np.tile(np.arange(2), 4), 16)
    o = {}
    x = np.asarray(i["x"]).reshape(2, HB, SEQ, 4, 16)[:, :, :LEN[0]]
    o["x"] = np.ascontiguousarray(x.transpose(3, 0, 4, 1, 2).reshape(128, HB * LEN[0]))
    w = np.zeros((128, LAYERS, 3, 128), f)
    for l in range(LAYERS):
        wd = np.asarray(i["L0_tok_W_dbc"][l])
        for s in range(2):
            rows = half_of == s
            for part, block in ((0, wd[1:65]), (1, wd[65:129])):
                w[rows, l, part, 64 * s:64 * s + 64] = chan(block.T)[rows]
            w[np.ix_(rows, [l], [2], rows)] = chan(wd[0])[rows][:, None, None, None]
    o["w_ssm"] = w
    v = np.zeros((128, LAYERS, 2), f)
    o["skip_w"] = np.zeros((128, LAYERS, 128), f)
    for l in range(LAYERS):
        v[:, l, 0] = chan(i["L0_tok_W_dt"][l][:, 0])
        v[:, l, 1] = chan(i["L0_tok_b_dt"][l])
        o["skip_w"][np.arange(128), l, np.arange(128)] = chan(i["L0_tok_D"][l])
    o["vecs"] = v
    al = np.asarray(i["L0_tok_A_log"]).transpose(2, 0, 1)
    o["a_log"] = np.concatenate([al, al], axis=0)
    wq = np.asarray(i["L0_attn_wqv_w"]).reshape(3, 4, 2, D, D)
    o["w_q"] = np.zeros((128, 2, NHP, 128), f)
    o["w_v"] = np.zeros((128, 2, 4, 2, 2, D), f)
    wv = np.asarray(i["L0_attn_wqv_w"]).reshape(3, 2, 4, D, D)[1:]
    o["w_e1"] = np.zeros((128, 2, NE // 2, 128), f)
    o["w_r1"] = np.zeros((128, 2, 32), f)
    o["w_fan"] = np.zeros((2, D, 128), f)
    for s in range(2):
        rows = half_of == s
        o["w_q"][rows, s] = chan(wq[0].transpose(3, 0, 1, 2).reshape(D, NHP, 128))[rows]
        o["w_v"][rows, s] = chan(wv.transpose(4, 2, 0, 1, 3))[rows]
        o["w_e1"][rows, s] = chan(np.asarray(i["L0_ffn_expert_w1"]).transpose(1, 0, 2).reshape(D, NE // 2, 128))[rows]
        o["w_r1"][rows, s] = chan(i["L0_ffn_router_w1"])[rows]
        o["w_fan"][s][:, rows] = chan(i["L0_attn_fanin_w"])[rows].T
    o["w_v"] = o["w_v"].reshape(128, 2, 4, 256)
    o["w_r1"] = o["w_r1"].reshape(128, 64)
    o["w_fan"] = o["w_fan"].reshape(128, 128)
    bq = np.asarray(i["L0_attn_wqv_b"]).reshape(3, 4, 128)
    o["b_q"] = bq[0].T
    o["w_k"] = np.asarray(i["L0_attn_wk"]).reshape(4, 128).T
    bv = np.asarray(i["L0_attn_wqv_b"]).reshape(3, 2, 4, 1, D)[1:].transpose(2, 3, 0, 1, 4)
    o["b_v"] = np.broadcast_to(bv, (4, 32, 2, 2, D)).reshape(128, 256)
    o["b_fan"] = chan(i["L0_attn_fanin_b"])[:, None]
    o["b_r1"] = np.tile(np.asarray(i["L0_ffn_router_b1"]), 2)[:, None]
    o["w_r2"] = np.zeros((2, 32, 2, NE), f)
    for s in range(2):
        o["w_r2"][s, :, s] = i["L0_ffn_router_w2"]
    o["w_r2"] = o["w_r2"].reshape(64, 2 * NE)
    o["b_r2"] = np.broadcast_to(np.asarray(i["L0_ffn_router_b2"]), (TT, NE))
    for n in (2, 3):
        w = np.zeros((2, D, NE // 2, 2, D), f)
        for e in range(NE):
            w[e % 2, :, e // 2, e % 2] = i[f"L0_ffn_expert_w{n}"][e]
        o[f"w_e{n}"] = w.reshape(128, NE // 2, 128)
    for n in (1, 2):
        o[f"b_e{n}"] = np.asarray(i[f"L0_ffn_expert_b{n}"]).reshape(NE // 2, 128).T
    o["b_e3"] = np.broadcast_to(np.asarray(i["L0_ffn_expert_b3"]).reshape(1, NE * D), (TT, NE * D))
    return o


def constants():
    f = np.float32
    o = {}
    s = np.zeros((2, 64, 16, 2, 16), f)
    for h in range(2):
        for el in range(16):
            s[h, :, el, h, el] = 1.0
    o["sel_red"] = s.reshape(128, 16, 32)
    o["neg_id"] = -np.eye(128, dtype=f).astype(np.dtype("bfloat16"))
    b = np.zeros((3, 2, 16, 16, 2, 64), f)
    for h in range(2):
        for el in range(16):
            b[:, h, el, el, h, :] = 1.0
    o["sel_bc"] = b.reshape(96, 16, 128).astype(np.dtype("bfloat16"))
    half_of = np.repeat(np.tile(np.arange(2), 4), 16)
    chan_of = (np.arange(4)[:, None, None] * 16 + np.zeros((1, 2, 1), int) + np.arange(16)).reshape(128)
    o["mean_w"] = ((half_of[:, None] == half_of[None, :]) / D).astype(f)
    o["ident"] = np.eye(128, dtype=f)
    o["sel_k"] = np.stack([((half_of == s)[:, None] & (chan_of[:, None] == np.tile(np.arange(D), 2)[None, :])) for s in range(2)], axis=1).astype(f)
    k = np.zeros((2, D, T, 2, 32), f)
    for h in range(2):
        for t in range(T):
            k[h, :, t, h, t] = 1.0
    o["sel_key"] = k.reshape(128, T, 64)
    o["key_rows"] = (np.arange(128) % 32 < T).astype(f)[:, None]
    own, other = np.meshgrid(np.arange(NE), np.arange(NE), indexing="ij")
    o["lower"] = np.broadcast_to(np.stack([other < own, other > own]).astype(f), (TT, 2, NE, NE))
    return o


def kernel(**inputs):
    import concourse.bacc as _bacc
    from concourse import mybir as _mybir
    from concourse.bass_utils import run_bass_kernel_spmd as _run
    nc = _bacc.Bacc("TRN2", target_bir_lowering=False, num_devices=1)
    arrays = {k: np.ascontiguousarray(v) for k, v in {**lay_out(inputs), **constants()}.items()}
    d = {k: nc.dram_tensor("in_" + k, a.shape, _mybir.dt.from_np(a.dtype), kind="ExternalInput").ap() for k, a in arrays.items()}
    out = nc.dram_tensor("out", (TT, 16, D), _mybir.dt.float32, kind="ExternalOutput").ap()
    build(nc, d, out)
    r = _run(nc, [{"in_" + k: a for k, a in arrays.items()}], core_ids=[0])
    o = r.results[0]["out"].reshape(4, T, 8, 2, D)
    return np.ascontiguousarray(o.transpose(3, 2, 0, 1, 4).reshape(BATCH, T, D))
```
